# Optimizing a Trainium2 kernel written in Bass

```python
import numpy as np
import jax
import jax.numpy as jnp

def _softmax(x, axis=-1):
    return jax.nn.softmax(x, axis=axis)
def _gelu(x):
    return jax.nn.gelu(x, approximate=True)
def _silu(x):
    return jax.nn.silu(x)
def _sigmoid(x):
    return jax.nn.sigmoid(x)
def _layernorm(x, axis=-1, eps=1e-5):
    m = jnp.mean(x, axis=axis, keepdims=True)
    v = jnp.var(x, axis=axis, keepdims=True)
    return (x - m) / jnp.sqrt(v + eps)
def _scatter_add(tgt, idx, src, axis=0):
    return tgt.at[idx].add(src)
def _segment_sum(src, seg, n):
    return jax.ops.segment_sum(src, seg, n)

kernel_name = 'mk_conv_attn_hybrid_d4_conv_nhwc128_d0c0c3'

def setup_inputs(seed: int = 0):
    np.random.seed(seed)
    _w = jnp.asarray
    def _rec_inputs():
        import jax
        import jax.numpy as jnp
        _gk = jax.random.key(seed)
        x = -0.0005207 + 1.001 * jax.random.normal(jax.random.fold_in(_gk, 1), (4, 64, 64, 128), jnp.float32)
        return x
    x = _rec_inputs()
    def _L0_conv_setup():
        import jax, jax.numpy as jnp
        import numpy as np
        B, H, W = (4, 64, 64)
        D_MODEL, D_STATE, D_CONV, EXPAND = (128, 16, 3, 2)
        D_INNER = EXPAND * D_MODEL
        DT_RANK = D_MODEL // 16
        LN_EPS = 1e-05

        def _selective_scan(u, delta, A, Bm, Cm, Dp, delta_bias):
            delta = jax.nn.softplus(delta + delta_bias[None, :, None])
            u_t = jnp.moveaxis(u, 2, 0)
            d_t = jnp.moveaxis(delta, 2, 0)
            B_t = jnp.moveaxis(Bm, 2, 0)
            C_t = jnp.moveaxis(Cm, 2, 0)

            def step(h, inp):
                u_i, d_i, b_i, c_i = inp
                dA = jnp.exp(d_i[..., None] * A)
                h = h * dA + (d_i * u_i)[..., None] * b_i[:, None, :]
                y = jnp.einsum('gdn,gn->gd', h, c_i)
                return (h, y)
            h0 = jnp.zeros((u.shape[0], u.shape[1], A.shape[1]), u.dtype)
            _, ys = jax.lax.scan(step, h0, (u_t, d_t, B_t, C_t))
            return jnp.moveaxis(ys, 0, 2) + u * Dp[None, :, None]

        def _forward(x, w_in, conv_w, conv_b, w_xproj, w_dt, b_dt, A_log, D_param, ln_w, ln_b, w_out):
            b, h, w, _ = x.shape
            L = h * w
            xz = x @ w_in
            xc, z = jnp.split(xz, 2, axis=-1)
            pad = (D_CONV - 1) // 2
            xc = jax.lax.conv_general_dilated(xc, conv_w, window_strides=(1, 1), padding=[(pad, pad), (pad, pad)], feature_group_count=D_INNER, dimension_numbers=('NHWC', 'HWIO', 'NHWC')) + conv_b
            xa = jax.nn.silu(xc)
            x_flat = xa.reshape(b, L, D_INNER)
            x_dbl = x_flat @ w_xproj
            dts, Bp, Cp = jnp.split(x_dbl, [DT_RANK, DT_RANK + D_STATE], axis=-1)
            dts = dts @ w_dt
            x_t = jnp.transpose(xa, (0, 2, 1, 3)).reshape(b, L, D_INNER)
            xs = jnp.stack([x_flat, x_t, jnp.flip(x_flat, 1), jnp.flip(x_t, 1)], axis=1)
            xs = xs.reshape(b * 4, L, D_INNER).transpose(0, 2, 1)

            def rep4(t):
                return jnp.broadcast_to(t[:, None], (b, 4) + t.shape[1:]).reshape((b * 4,) + t.shape[1:]).transpose(0, 2, 1)
            dts4, Bp4, Cp4 = (rep4(dts), rep4(Bp), rep4(Cp))
            A = -jnp.exp(A_log.astype(jnp.float32))
            ys = _selective_scan(xs, dts4, A, Bp4, Cp4, D_param.astype(jnp.float32), b_dt.astype(jnp.float32))
            ys = ys.transpose(0, 2, 1).reshape(b, 4, L, D_INNER)
            y = ys[:, 0].reshape(b, h, w, D_INNER) + jnp.transpose(ys[:, 1].reshape(b, w, h, D_INNER), (0, 2, 1, 3)) + jnp.flip(ys[:, 2], 1).reshape(b, h, w, D_INNER) + jnp.transpose(jnp.flip(ys[:, 3], 1).reshape(b, w, h, D_INNER), (0, 2, 1, 3))
            mu = jnp.mean(y, axis=-1, keepdims=True)
            var = jnp.mean(jnp.square(y - mu), axis=-1, keepdims=True)
            y = (y - mu) * jax.lax.rsqrt(var + LN_EPS) * ln_w + ln_b
            y = y * jax.nn.silu(z)
            return y @ w_out
        key = jax.random.key(seed)
        ks = jax.random.split(key, 9)
        s = 0.02
        x = jax.random.normal(ks[0], (B, H, W, D_MODEL), dtype=jnp.float32)
        w_in = jax.random.normal(ks[1], (D_MODEL, 2 * D_INNER), dtype=jnp.float32) * s
        conv_w = jax.random.normal(ks[2], (D_CONV, D_CONV, 1, D_INNER), dtype=jnp.float32) * s
        conv_b = jax.random.normal(ks[3], (D_INNER,), dtype=jnp.float32) * s
        w_xproj = jax.random.normal(ks[4], (D_INNER, DT_RANK + 2 * D_STATE), dtype=jnp.float32) * s
        w_dt = jax.random.normal(ks[5], (DT_RANK, D_INNER), dtype=jnp.float32) * s
        b_dt = jax.random.normal(ks[6], (D_INNER,), dtype=jnp.float32) * s
        A_log = jnp.log(jnp.broadcast_to(jnp.arange(1, D_STATE + 1, dtype=jnp.float32), (D_INNER, D_STATE)))
        D_param = jnp.ones((D_INNER,), dtype=jnp.float32)
        ln_w = jnp.ones((D_INNER,), dtype=jnp.float32)
        ln_b = jnp.zeros((D_INNER,), dtype=jnp.float32)
        w_out = jax.random.normal(ks[7], (D_INNER, D_MODEL), dtype=jnp.float32) * s
        return {'x': x, 'w_in': w_in, 'conv_w': conv_w, 'conv_b': conv_b, 'w_xproj': w_xproj, 'w_dt': w_dt, 'b_dt': b_dt, 'A_log': A_log, 'D_param': D_param, 'ln_w': ln_w, 'ln_b': ln_b, 'w_out': w_out}
    _L0_conv_all = _L0_conv_setup()
    _L0_conv_in = {k: v for k, v in _L0_conv_all.items() if k in ('w_in', 'conv_w', 'conv_b', 'w_xproj', 'w_dt', 'b_dt', 'A_log', 'D_param', 'ln_w', 'ln_b', 'w_out', )}
    del _L0_conv_all

    def _L1_conv_setup():
        import jax, jax.numpy as jnp
        import numpy as np
        import math
        D_MODEL = 128
        D_STATE = 16
        D_CONV = 3
        EXPAND = 2
        D_INNER = EXPAND * D_MODEL
        DT_RANK = math.ceil(D_MODEL / 16)
        B, H, W = (2, 64, 64)
        LN_EPS = 1e-05

        def _local_scan(x, Hh, Ww, w_h, w_w, flip=False, column_first=False):
            Bb, C = (x.shape[0], x.shape[1])
            Hg, Wg = (Hh // w_h, Ww // w_w)
            x = x.reshape(Bb, C, Hg, w_h, Wg, w_w)
            if column_first:
                x = x.transpose(0, 1, 4, 2, 5, 3)
            else:
                x = x.transpose(0, 1, 2, 4, 3, 5)
            x = x.reshape(Bb, C, -1)
            if flip:
                x = x[:, :, ::-1]
            return x

        def _selective_scan(u, delta, A, Bm, Cm, D, delta_bias):
            Bsz, Dch, L = u.shape
            K, N = (Bm.shape[1], A.shape[1])
            d = Dch // K
            delta = jax.nn.softplus(delta + delta_bias[None, :, None])
            A4 = A.reshape(K, d, N)
            u4 = u.reshape(Bsz, K, d, L)
            dt4 = delta.reshape(Bsz, K, d, L)

            def step(h, inp):
                ut, dt, bt, ct = inp
                dA = jnp.exp(dt[..., None] * A4)
                h = dA * h + (dt * ut)[..., None] * bt[:, :, None, :]
                y = jnp.einsum('bkdn,bkn->bkd', h, ct)
                return (h, y)
            xs_t = (u4.transpose(3, 0, 1, 2), dt4.transpose(3, 0, 1, 2), Bm.transpose(3, 0, 1, 2), Cm.transpose(3, 0, 1, 2))
            h0 = jnp.zeros((Bsz, K, d, N), u.dtype)
            _, ys = jax.lax.scan(step, h0, xs_t)
            y = ys.transpose(1, 2, 3, 0).reshape(Bsz, Dch, L)
            return y + u * D[None, :, None]
        key = jax.random.key(seed)
        ks = jax.random.split(key, 8)
        x = jax.random.normal(ks[0], (B, H, W, D_MODEL), jnp.float32)
        W_in = jax.random.normal(ks[1], (2 * D_INNER, D_MODEL), jnp.float32) * D_MODEL ** (-0.5)
        conv_w = jax.random.normal(ks[2], (D_INNER, 1, D_CONV, D_CONV), jnp.float32) * (1.0 / D_CONV)
        conv_b = jnp.zeros((D_INNER,), jnp.float32)
        x_proj_w = jax.random.normal(ks[3], (4, DT_RANK + 2 * D_STATE, D_INNER), jnp.float32) * D_INNER ** (-0.5)
        std = DT_RANK ** (-0.5)
        dt_proj_w = jax.random.uniform(ks[4], (4, D_INNER, DT_RANK), jnp.float32, -std, std)
        dt = jnp.exp(jax.random.uniform(ks[5], (4, D_INNER), jnp.float32) * (math.log(0.1) - math.log(0.001)) + math.log(0.001))
        dt = jnp.maximum(dt, 0.0001)
        dt_proj_b = dt + jnp.log(-jnp.expm1(-dt))
        A_logs = jnp.log(jnp.tile(jnp.arange(1, D_STATE + 1, dtype=jnp.float32)[None, :], (4 * D_INNER, 1)))
        Ds = jnp.ones((4 * D_INNER,), jnp.float32)
        ln_w = jnp.ones((D_INNER,), jnp.float32)
        ln_b = jnp.zeros((D_INNER,), jnp.float32)
        W_out = jax.random.normal(ks[6], (D_MODEL, D_INNER), jnp.float32) * D_INNER ** (-0.5)
        return dict(x=x, W_in=W_in, conv_w=conv_w, conv_b=conv_b, x_proj_w=x_proj_w, dt_proj_w=dt_proj_w, dt_proj_b=dt_proj_b, A_logs=A_logs, Ds=Ds, ln_w=ln_w, ln_b=ln_b, W_out=W_out)
    _L1_conv_all = _L1_conv_setup()
    _L1_conv_in = {k: v for k, v in _L1_conv_all.items() if k in ('W_in', 'conv_w', 'conv_b', 'x_proj_w', 'dt_proj_w', 'dt_proj_b', 'A_logs', 'Ds', 'ln_w', 'ln_b', 'W_out', )}
    del _L1_conv_all

    def _L2_attn_setup():
        import jax, jax.numpy as jnp
        import numpy as np
        B, S, H, A = (8, 1024, 128, 16)
        key = jax.random.key(seed)
        ks = jax.random.split(key, 5)
        scale = 1.0 / np.sqrt(2 * H)
        return {'x': jax.random.normal(ks[0], (B, S, H), dtype=jnp.float32), 'W1': jax.random.normal(ks[1], (2 * H, A), dtype=jnp.float32) * scale, 'b1': jax.random.normal(ks[2], (A,), dtype=jnp.float32) * scale, 'w2': jax.random.normal(ks[3], (A, 1), dtype=jnp.float32) * (1.0 / np.sqrt(A)), 'b2': jax.random.normal(ks[4], (1,), dtype=jnp.float32) * (1.0 / np.sqrt(A))}
    _L2_attn_all = _L2_attn_setup()
    _L2_attn_in = {k: v for k, v in _L2_attn_all.items() if k in ('W1', 'b1', 'w2', 'b2', )}
    del _L2_attn_all

    def _L2_ffn_setup():
        import jax, jax.numpy as jnp
        import numpy as np
        B, S, D, E, H, O, K = (512, 2048, 128, 64, 512, 128, 8)
        key = jax.random.key(seed)
        k0, k1, k2, k3 = jax.random.split(key, 4)
        x = jax.random.normal(k0, (B, S, D), dtype=jnp.float32)
        gate_w = jax.random.normal(k1, (E, D), dtype=jnp.float32) * (1.0 / np.sqrt(D))
        gate_b = jnp.zeros((E,), dtype=jnp.float32)
        weight1 = jax.random.uniform(k2, (E, D + 1, H), dtype=jnp.float32, minval=-1.0, maxval=1.0) * (1.0 / np.sqrt(D + 1))
        weight2 = jax.random.uniform(k3, (E, H + 1, O), dtype=jnp.float32, minval=-1.0, maxval=1.0) * (1.0 / np.sqrt(H + 1))
        return {'x': x, 'gate_w': gate_w, 'gate_b': gate_b, 'weight1': weight1, 'weight2': weight2}
    _L2_ffn_all = _L2_ffn_setup()
    _L2_ffn_in = {k: v for k, v in _L2_ffn_all.items() if k in ('gate_w', 'gate_b', 'weight1', 'weight2', )}
    del _L2_ffn_all

    def _L3_attn_setup():
        import jax, jax.numpy as jnp
        import numpy as np
        B, N, D = (4, 1024, 128)
        key = jax.random.key(seed)
        ks = jax.random.split(key, 4)
        scale = 1.0 / np.sqrt(D)
        return {'inputs': jax.random.normal(ks[0], (B, N, D), dtype=jnp.float32), 'Wq': jax.random.normal(ks[1], (D, D), dtype=jnp.float32) * scale, 'bq': jnp.zeros((D,), dtype=jnp.float32), 'Wk': jax.random.normal(ks[2], (D, D), dtype=jnp.float32) * scale, 'bk': jnp.zeros((D,), dtype=jnp.float32), 'Wv': jax.random.normal(ks[3], (D, D), dtype=jnp.float32) * scale, 'bv': jnp.zeros((D,), dtype=jnp.float32)}
    _L3_attn_all = _L3_attn_setup()
    _L3_attn_in = {k: v for k, v in _L3_attn_all.items() if k in ('Wq', 'bq', 'Wk', 'bk', 'Wv', 'bv', )}
    del _L3_attn_all

    def _L3_ffn_setup():
        import jax, jax.numpy as jnp
        import numpy as np
        B, S, D, E, H, O, K = (512, 2048, 128, 64, 512, 128, 8)
        key = jax.random.key(seed)
        k0, k1, k2, k3 = jax.random.split(key, 4)
        x = jax.random.normal(k0, (B, S, D), dtype=jnp.float32)
        gate_w = jax.random.normal(k1, (E, D), dtype=jnp.float32) * (1.0 / np.sqrt(D))
        gate_b = jnp.zeros((E,), dtype=jnp.float32)
        weight1 = jax.random.uniform(k2, (E, D + 1, H), dtype=jnp.float32, minval=-1.0, maxval=1.0) * (1.0 / np.sqrt(D + 1))
        weight2 = jax.random.uniform(k3, (E, H + 1, O), dtype=jnp.float32, minval=-1.0, maxval=1.0) * (1.0 / np.sqrt(H + 1))
        return {'x': x, 'gate_w': gate_w, 'gate_b': gate_b, 'weight1': weight1, 'weight2': weight2}
    _L3_ffn_all = _L3_ffn_setup()
    _L3_ffn_in = {k: v for k, v in _L3_ffn_all.items() if k in ('gate_w', 'gate_b', 'weight1', 'weight2', )}
    del _L3_ffn_all

    return {
        "x": x,
        "L0_conv_w_in": _L0_conv_in["w_in"],
        "L0_conv_conv_w": _L0_conv_in["conv_w"],
        "L0_conv_conv_b": _L0_conv_in["conv_b"],
        "L0_conv_w_xproj": _L0_conv_in["w_xproj"],
        "L0_conv_w_dt": _L0_conv_in["w_dt"],
        "L0_conv_b_dt": _L0_conv_in["b_dt"],
        "L0_conv_A_log": _L0_conv_in["A_log"],
        "L0_conv_D_param": _L0_conv_in["D_param"],
        "L0_conv_ln_w": _L0_conv_in["ln_w"],
        "L0_conv_ln_b": _L0_conv_in["ln_b"],
        "L0_conv_w_out": _L0_conv_in["w_out"],
        "L1_conv_W_in": _L1_conv_in["W_in"],
        "L1_conv_conv_w": _L1_conv_in["conv_w"],
        "L1_conv_conv_b": _L1_conv_in["conv_b"],
        "L1_conv_x_proj_w": _L1_conv_in["x_proj_w"],
        "L1_conv_dt_proj_w": _L1_conv_in["dt_proj_w"],
        "L1_conv_dt_proj_b": _L1_conv_in["dt_proj_b"],
        "L1_conv_A_logs": _L1_conv_in["A_logs"],
        "L1_conv_Ds": _L1_conv_in["Ds"],
        "L1_conv_ln_w": _L1_conv_in["ln_w"],
        "L1_conv_ln_b": _L1_conv_in["ln_b"],
        "L1_conv_W_out": _L1_conv_in["W_out"],
        "L2_attn_W1": _L2_attn_in["W1"],
        "L2_attn_b1": _L2_attn_in["b1"],
        "L2_attn_w2": _L2_attn_in["w2"],
        "L2_attn_b2": _L2_attn_in["b2"],
        "L2_ffn_gate_w": _L2_ffn_in["gate_w"],
        "L2_ffn_gate_b": _L2_ffn_in["gate_b"],
        "L2_ffn_weight1": _L2_ffn_in["weight1"],
        "L2_ffn_weight2": _L2_ffn_in["weight2"],
        "L3_attn_Wq": _L3_attn_in["Wq"],
        "L3_attn_bq": _L3_attn_in["bq"],
        "L3_attn_Wk": _L3_attn_in["Wk"],
        "L3_attn_bk": _L3_attn_in["bk"],
        "L3_attn_Wv": _L3_attn_in["Wv"],
        "L3_attn_bv": _L3_attn_in["bv"],
        "L3_ffn_gate_w": _L3_ffn_in["gate_w"],
        "L3_ffn_gate_b": _L3_ffn_in["gate_b"],
        "L3_ffn_weight1": _L3_ffn_in["weight1"],
        "L3_ffn_weight2": _L3_ffn_in["weight2"],
    }

def reference(x, L0_conv_w_in, L0_conv_conv_w, L0_conv_conv_b, L0_conv_w_xproj, L0_conv_w_dt, L0_conv_b_dt, L0_conv_A_log, L0_conv_D_param, L0_conv_ln_w, L0_conv_ln_b, L0_conv_w_out, L1_conv_W_in, L1_conv_conv_w, L1_conv_conv_b, L1_conv_x_proj_w, L1_conv_dt_proj_w, L1_conv_dt_proj_b, L1_conv_A_logs, L1_conv_Ds, L1_conv_ln_w, L1_conv_ln_b, L1_conv_W_out, L2_attn_W1, L2_attn_b1, L2_attn_w2, L2_attn_b2, L2_ffn_gate_w, L2_ffn_gate_b, L2_ffn_weight1, L2_ffn_weight2, L3_attn_Wq, L3_attn_bq, L3_attn_Wk, L3_attn_bk, L3_attn_Wv, L3_attn_bv, L3_ffn_gate_w, L3_ffn_gate_b, L3_ffn_weight1, L3_ffn_weight2):
    import jax
    import jax.numpy as jnp
    def _L0_conv_ref(x, w_in, conv_w, conv_b, w_xproj, w_dt, b_dt, A_log, D_param, ln_w, ln_b, w_out):
        import jax, jax.numpy as jnp
        import numpy as np
        B, H, W = (4, 64, 64)
        D_MODEL, D_STATE, D_CONV, EXPAND = (128, 16, 3, 2)
        D_INNER = EXPAND * D_MODEL
        DT_RANK = D_MODEL // 16
        LN_EPS = 1e-05

        def _selective_scan(u, delta, A, Bm, Cm, Dp, delta_bias):
            delta = jax.nn.softplus(delta + delta_bias[None, :, None])
            u_t = jnp.moveaxis(u, 2, 0)
            d_t = jnp.moveaxis(delta, 2, 0)
            B_t = jnp.moveaxis(Bm, 2, 0)
            C_t = jnp.moveaxis(Cm, 2, 0)

            def step(h, inp):
                u_i, d_i, b_i, c_i = inp
                dA = jnp.exp(d_i[..., None] * A)
                h = h * dA + (d_i * u_i)[..., None] * b_i[:, None, :]
                y = jnp.einsum('gdn,gn->gd', h, c_i)
                return (h, y)
            h0 = jnp.zeros((u.shape[0], u.shape[1], A.shape[1]), u.dtype)
            _, ys = jax.lax.scan(step, h0, (u_t, d_t, B_t, C_t))
            return jnp.moveaxis(ys, 0, 2) + u * Dp[None, :, None]

        def _forward(x, w_in, conv_w, conv_b, w_xproj, w_dt, b_dt, A_log, D_param, ln_w, ln_b, w_out):
            b, h, w, _ = x.shape
            L = h * w
            xz = x @ w_in
            xc, z = jnp.split(xz, 2, axis=-1)
            pad = (D_CONV - 1) // 2
            xc = jax.lax.conv_general_dilated(xc, conv_w, window_strides=(1, 1), padding=[(pad, pad), (pad, pad)], feature_group_count=D_INNER, dimension_numbers=('NHWC', 'HWIO', 'NHWC')) + conv_b
            xa = jax.nn.silu(xc)
            x_flat = xa.reshape(b, L, D_INNER)
            x_dbl = x_flat @ w_xproj
            dts, Bp, Cp = jnp.split(x_dbl, [DT_RANK, DT_RANK + D_STATE], axis=-1)
            dts = dts @ w_dt
            x_t = jnp.transpose(xa, (0, 2, 1, 3)).reshape(b, L, D_INNER)
            xs = jnp.stack([x_flat, x_t, jnp.flip(x_flat, 1), jnp.flip(x_t, 1)], axis=1)
            xs = xs.reshape(b * 4, L, D_INNER).transpose(0, 2, 1)

            def rep4(t):
                return jnp.broadcast_to(t[:, None], (b, 4) + t.shape[1:]).reshape((b * 4,) + t.shape[1:]).transpose(0, 2, 1)
            dts4, Bp4, Cp4 = (rep4(dts), rep4(Bp), rep4(Cp))
            A = -jnp.exp(A_log.astype(jnp.float32))
            ys = _selective_scan(xs, dts4, A, Bp4, Cp4, D_param.astype(jnp.float32), b_dt.astype(jnp.float32))
            ys = ys.transpose(0, 2, 1).reshape(b, 4, L, D_INNER)
            y = ys[:, 0].reshape(b, h, w, D_INNER) + jnp.transpose(ys[:, 1].reshape(b, w, h, D_INNER), (0, 2, 1, 3)) + jnp.flip(ys[:, 2], 1).reshape(b, h, w, D_INNER) + jnp.transpose(jnp.flip(ys[:, 3], 1).reshape(b, w, h, D_INNER), (0, 2, 1, 3))
            mu = jnp.mean(y, axis=-1, keepdims=True)
            var = jnp.mean(jnp.square(y - mu), axis=-1, keepdims=True)
            y = (y - mu) * jax.lax.rsqrt(var + LN_EPS) * ln_w + ln_b
            y = y * jax.nn.silu(z)
            return y @ w_out
        return _forward(x, w_in, conv_w, conv_b, w_xproj, w_dt, b_dt, A_log, D_param, ln_w, ln_b, w_out)

    def _L1_conv_ref(x, W_in, conv_w, conv_b, x_proj_w, dt_proj_w, dt_proj_b, A_logs, Ds, ln_w, ln_b, W_out):
        import jax, jax.numpy as jnp
        import numpy as np
        import math
        D_MODEL = 128
        D_STATE = 16
        D_CONV = 3
        EXPAND = 2
        D_INNER = EXPAND * D_MODEL
        DT_RANK = math.ceil(D_MODEL / 16)
        B, H, W = (2, 64, 64)
        LN_EPS = 1e-05

        def _local_scan(x, Hh, Ww, w_h, w_w, flip=False, column_first=False):
            Bb, C = (x.shape[0], x.shape[1])
            Hg, Wg = (Hh // w_h, Ww // w_w)
            x = x.reshape(Bb, C, Hg, w_h, Wg, w_w)
            if column_first:
                x = x.transpose(0, 1, 4, 2, 5, 3)
            else:
                x = x.transpose(0, 1, 2, 4, 3, 5)
            x = x.reshape(Bb, C, -1)
            if flip:
                x = x[:, :, ::-1]
            return x

        def _selective_scan(u, delta, A, Bm, Cm, D, delta_bias):
            Bsz, Dch, L = u.shape
            K, N = (Bm.shape[1], A.shape[1])
            d = Dch // K
            delta = jax.nn.softplus(delta + delta_bias[None, :, None])
            A4 = A.reshape(K, d, N)
            u4 = u.reshape(Bsz, K, d, L)
            dt4 = delta.reshape(Bsz, K, d, L)

            def step(h, inp):
                ut, dt, bt, ct = inp
                dA = jnp.exp(dt[..., None] * A4)
                h = dA * h + (dt * ut)[..., None] * bt[:, :, None, :]
                y = jnp.einsum('bkdn,bkn->bkd', h, ct)
                return (h, y)
            xs_t = (u4.transpose(3, 0, 1, 2), dt4.transpose(3, 0, 1, 2), Bm.transpose(3, 0, 1, 2), Cm.transpose(3, 0, 1, 2))
            h0 = jnp.zeros((Bsz, K, d, N), u.dtype)
            _, ys = jax.lax.scan(step, h0, xs_t)
            y = ys.transpose(1, 2, 3, 0).reshape(Bsz, Dch, L)
            return y + u * D[None, :, None]
        Bb, Hh, Ww, _ = x.shape
        L = Hh * Ww
        d_inner = conv_b.shape[0]
        dt_rank = dt_proj_w.shape[2]
        N = A_logs.shape[1]
        xz = x @ W_in.T
        xc, z = jnp.split(xz, 2, axis=-1)
        xc = xc.transpose(0, 3, 1, 2)
        xc = jax.lax.conv_general_dilated(xc, conv_w, (1, 1), ((1, 1), (1, 1)), dimension_numbers=('NCHW', 'OIHW', 'NCHW'), feature_group_count=d_inner) + conv_b[None, :, None, None]
        xc = jax.nn.silu(xc)
        w_h, w_w = (Hh // 4, Ww // 4)
        x1 = _local_scan(xc, Hh, Ww, w_h, w_w)
        x2 = _local_scan(xc, Hh, Ww, w_h, w_w, column_first=True)
        x3 = _local_scan(xc, Hh, Ww, w_h, w_w, flip=True)
        x4 = _local_scan(xc, Hh, Ww, w_h, w_w, column_first=True, flip=True)
        xs = jnp.stack([x1, x2, x3, x4], axis=1)
        x_dbl = jnp.einsum('bkdl,kcd->bkcl', xs, x_proj_w)
        dts, Bs, Cs = jnp.split(x_dbl, [dt_rank, dt_rank + N], axis=2)
        dts = jnp.einsum('bkrl,kdr->bkdl', dts, dt_proj_w)
        u = xs.reshape(Bb, -1, L)
        delta = dts.reshape(Bb, -1, L)
        As = -jnp.exp(A_logs)
        out_y = _selective_scan(u, delta, As, Bs, Cs, Ds, dt_proj_b.reshape(-1)).reshape(Bb, 4, -1, L)
        inv_y = out_y[:, 2:4, :, ::-1]
        wh_y = out_y[:, 1].reshape(Bb, -1, Ww, Hh).transpose(0, 1, 3, 2).reshape(Bb, -1, L)
        invwh_y = inv_y[:, 1].reshape(Bb, -1, Ww, Hh).transpose(0, 1, 3, 2).reshape(Bb, -1, L)
        y = out_y[:, 0] + inv_y[:, 0] + wh_y + invwh_y
        y = y.transpose(0, 2, 1).reshape(Bb, Hh, Ww, -1)
        mu = jnp.mean(y, axis=-1, keepdims=True)
        var = jnp.mean(jnp.square(y - mu), axis=-1, keepdims=True)
        y = (y - mu) * jax.lax.rsqrt(var + LN_EPS) * ln_w + ln_b
        y = y * jax.nn.silu(z)
        return y @ W_out.T

    def _L2_attn_ref(x, W1, b1, w2, b2):
        import jax, jax.numpy as jnp
        import numpy as np
        B, S, H, A = (8, 1024, 128, 16)
        h = x.shape[-1]
        f = jnp.einsum('bih,ha->bia', x, W1[:h])
        g = jnp.einsum('bjh,ha->bja', x, W1[h:])
        t = jnp.tanh(f[:, :, None, :] + g[:, None, :, :] + b1)
        scores = jnp.einsum('bija,a->bij', t, w2[:, 0]) + b2[0]
        n_seq = x.shape[1]
        flag = jnp.tril(jnp.ones((n_seq, n_seq), dtype=x.dtype), -1)[None, :, :]
        e = jnp.exp(scores) * flag
        denom = jnp.sum(e, axis=-1, keepdims=True) + 1e-10
        w = e / denom
        return jnp.einsum('bij,bjh->bih', w, x)

    def _L2_ffn_ref(x, gate_w, gate_b, weight1, weight2):
        import jax, jax.numpy as jnp
        import numpy as np
        B, S, D, E, H, O, K = (512, 2048, 128, 64, 512, 128, 8)
        Bn, Sn, Dn = x.shape
        logits = jnp.einsum('bsd,ed->bse', x, gate_w) + gate_b
        probs = jax.nn.softmax(logits, axis=1)
        vals, idx = jax.lax.top_k(probs.transpose(0, 2, 1), K)
        topv = vals.transpose(0, 2, 1)
        topi = idx.transpose(0, 2, 1)
        flat_idx = topi.reshape(Bn, K * E)
        gathered = jnp.take_along_axis(x, flat_idx[:, :, None], axis=1)
        gathered = gathered.reshape(Bn, K, E, Dn)
        pooled = jnp.einsum('bked,bke->bed', gathered, topv)
        ones = jnp.ones((E, Bn, 1), dtype=x.dtype)
        h = jnp.concatenate([pooled.transpose(1, 0, 2), ones], axis=-1)
        h = jax.nn.gelu(jnp.einsum('ebd,edh->ebh', h, weight1), approximate=False)
        h = jnp.concatenate([h, ones], axis=-1)
        out = jnp.einsum('ebh,eho->ebo', h, weight2)
        out = out.transpose(1, 0, 2)
        weighted = jnp.einsum('beo,bke->bkeo', out, topv).reshape(Bn, K * E, O)
        outputs = jnp.zeros((Bn, Sn, O), dtype=x.dtype)
        outputs = outputs.at[jnp.arange(Bn)[:, None], flat_idx].add(weighted)
        return outputs

    def _L3_attn_ref(inputs, Wq, bq, Wk, bk, Wv, bv):
        import jax, jax.numpy as jnp
        import numpy as np
        B, N, D = (4, 1024, 128)
        q = inputs @ Wq + bq
        k = inputs @ Wk + bk
        v = inputs @ Wv + bv
        kv = jnp.sum(k * v, axis=1, keepdims=True)
        return q * kv

    def _L3_ffn_ref(x, gate_w, gate_b, weight1, weight2):
        import jax, jax.numpy as jnp
        import numpy as np
        B, S, D, E, H, O, K = (512, 2048, 128, 64, 512, 128, 8)
        Bn, Sn, Dn = x.shape
        logits = jnp.einsum('bsd,ed->bse', x, gate_w) + gate_b
        probs = jax.nn.softmax(logits, axis=1)
        vals, idx = jax.lax.top_k(probs.transpose(0, 2, 1), K)
        topv = vals.transpose(0, 2, 1)
        topi = idx.transpose(0, 2, 1)
        flat_idx = topi.reshape(Bn, K * E)
        gathered = jnp.take_along_axis(x, flat_idx[:, :, None], axis=1)
        gathered = gathered.reshape(Bn, K, E, Dn)
        pooled = jnp.einsum('bked,bke->bed', gathered, topv)
        ones = jnp.ones((E, Bn, 1), dtype=x.dtype)
        h = jnp.concatenate([pooled.transpose(1, 0, 2), ones], axis=-1)
        h = jax.nn.gelu(jnp.einsum('ebd,edh->ebh', h, weight1), approximate=False)
        h = jnp.concatenate([h, ones], axis=-1)
        out = jnp.einsum('ebh,eho->ebo', h, weight2)
        out = out.transpose(1, 0, 2)
        weighted = jnp.einsum('beo,bke->bkeo', out, topv).reshape(Bn, K * E, O)
        outputs = jnp.zeros((Bn, Sn, O), dtype=x.dtype)
        outputs = outputs.at[jnp.arange(Bn)[:, None], flat_idx].add(weighted)
        return outputs

    def _gn(v, G=32, eps=1e-5):
        B_, H_, W_, C_ = v.shape
        g = v.reshape(B_, H_, W_, G, C_ // G)
        m = jnp.mean(g, axis=(1, 2, 4), keepdims=True)
        s = jnp.var(g, axis=(1, 2, 4), keepdims=True)
        return ((g - m) / jnp.sqrt(s + eps)).reshape(v.shape)

    def _ln_c(v, eps=1e-6):
        m = jnp.mean(v, axis=-1, keepdims=True)
        s = jnp.var(v, axis=-1, keepdims=True)
        return (v - m) / jnp.sqrt(s + eps)

    def _ln_t(v, eps=1e-5):
        m = jnp.mean(v, axis=-1, keepdims=True)
        s = jnp.var(v, axis=-1, keepdims=True)
        return (v - m) / jnp.sqrt(s + eps)

    def _to_tokens(v):
        B_, H_, W_, C_ = v.shape
        return v.reshape(B_, H_ * W_, C_)
    def _from_tokens(t, like):
        return t.reshape(like.shape)

    x = x + _L0_conv_ref(_gn(x), L0_conv_w_in, L0_conv_conv_w, L0_conv_conv_b, L0_conv_w_xproj, L0_conv_w_dt, L0_conv_b_dt, L0_conv_A_log, L0_conv_D_param, L0_conv_ln_w, L0_conv_ln_b, L0_conv_w_out)
    x = x + _L1_conv_ref(_gn(x), L1_conv_W_in, L1_conv_conv_w, L1_conv_conv_b, L1_conv_x_proj_w, L1_conv_dt_proj_w, L1_conv_dt_proj_b, L1_conv_A_logs, L1_conv_Ds, L1_conv_ln_w, L1_conv_ln_b, L1_conv_W_out)
    t = _to_tokens(x)
    t = t + _L2_attn_ref(_ln_t(t), L2_attn_W1, L2_attn_b1, L2_attn_w2, L2_attn_b2)
    t = t + _L2_ffn_ref(_ln_t(t), L2_ffn_gate_w, L2_ffn_gate_b, L2_ffn_weight1, L2_ffn_weight2)
    t = t + _L3_attn_ref(_ln_t(t), L3_attn_Wq, L3_attn_bq, L3_attn_Wk, L3_attn_bk, L3_attn_Wv, L3_attn_bv)
    t = t + _L3_ffn_ref(_ln_t(t), L3_ffn_gate_w, L3_ffn_gate_b, L3_ffn_weight1, L3_ffn_weight2)
    x = _from_tokens(t, x)
    return x


_drawn_inputs = setup_inputs


def setup_inputs(seed=0):
    import zlib

    import numpy as np

    out = dict(_drawn_inputs(seed))
    spreads = {'L0_conv_D_param': (1.0, 0.6),
     'L0_conv_ln_w': (1.0, 0.6),
     'L0_conv_ln_b': (0.0, 0.8),
     'L1_conv_conv_b': (0.0, 0.1),
     'L1_conv_Ds': (1.0, 0.2),
     'L1_conv_ln_w': (1.0, 0.2),
     'L1_conv_ln_b': (0.0, 0.1),
     'L2_ffn_gate_b': (0.0, 2.0),
     'L3_attn_bq': (0.0, 0.1),
     'L3_attn_bk': (0.0, 0.1),
     'L3_attn_bv': (0.0, 0.1),
     'L3_ffn_gate_b': (0.0, 0.1)}
    factors = {'L0_conv_w_xproj': 64.0,
     'L0_conv_w_dt': 64.0,
     'L0_conv_b_dt': 64.0,
     'L0_conv_A_log': 64.0,
     'L1_conv_dt_proj_w': 4.426,
     'L2_attn_b1': 35.008,
     'L2_ffn_gate_w': 8.0,
     'L2_ffn_weight1': 8.0,
     'L2_ffn_weight2': 8.0,
     'L3_ffn_gate_w': 64.0,
     'L3_ffn_weight1': 64.0,
     'L3_ffn_weight2': 64.0}
    for name, (base, spread) in spreads.items():
        noise = np.random.default_rng([zlib.crc32(name.encode()), seed]).standard_normal(out[name].shape)
        drawn = base * np.exp(spread * noise) if base else spread * noise
        out[name] = jnp.asarray(drawn.astype(out[name].dtype))
    for name, factor in factors.items():
        out[name] = (out[name] * factor).astype(out[name].dtype)
    return out
```

```python
import math
from contextlib import ExitStack

import concourse.bass as bass
from concourse import mybir

ALU = mybir.AluOpType
ACT = mybir.ActivationFunctionType
F32 = mybir.dt.float32
BF16 = mybir.dt.bfloat16

P = 128
L = 4096
W = 64
DI = 256
NS = 16
R = 8
T = 512
NCH = L // T
TILES = 2 * NS
K = 4
NH, NG, NC, ND = 8, 4, 4, 4
PW = W + 2
CR = 64
ROWS = T // W
NSPLIT = 96

A16, I8 = 16, 8
PASS = 2048
NT = 8
E64, HID, TOP = 64, 512, 8
EG = 4
LOWEST = -3.4028234663852886e38

Y0, A0, B0, CB, MB = 0, 2, 4, 6, 7


def program(nc, t, res, out, batches):
    ctx = ExitStack()

    def sb(name, shape, dt=F32):
        return ctx.enter_context(nc.sbuf_tensor(name, shape, dt))

    with ctx:
        ps = ctx.enter_context(nc.psum_tensor("ps", [P, 8, T], F32))
        counting = []

        def sem(name, credit=True):
            s = ctx.enter_context(nc.semaphore(name))
            if credit:
                counting.append(s)
            return s

        ds = bass.ds

        ident = sb("ident", [P, P])
        group_mean = sb("group_mean", [P, P])
        mean256 = sb("mean256", [P, P])
        mean128 = sb("mean128", [P, P])
        pick = sb("pick", [NSPLIT, 32], BF16)
        keep_mid = sb("keep_mid", [NSPLIT, 1])
        keep_low = sb("keep_low", [NSPLIT, 1])
        eps = sb("eps", [P, 2])
        lay = []
        for n, kk in ((0, 1), (1, K)):
            lay.append(dict(
                kk=kk,
                win=sb(f"win{n}", [P, 2 * DI]), cw=sb(f"cw{n}", [P, 2, 9]), cb=sb(f"cb{n}", [P, 2]),
                wx=sb(f"wx{n}", [P, kk, 2, NSPLIT + R]), wdt=sb(f"wdt{n}", [NSPLIT + R, kk, DI]),
                dtb=sb(f"dtb{n}", [P, kk, 2]), al=sb(f"al{n}", [P, kk, 2, NS]), na=sb(f"na{n}", [P, kk, 2, NS]),
                dd=sb(f"dd{n}", [P, kk, 2]), dsum=sb(f"dsum{n}", [P, 2, 2]),
                lw=sb(f"lw{n}", [P, 2]), lb=sb(f"lb{n}", [P, 2]), wo=sb(f"wo{n}", [P, 2, P])))

        xT = sb("xT", [P, L])
        V = sb("V", [P, 2, 2, L])
        ypad = sb("ypad", [P, 2, PW * PW])
        Y = ypad[:, :, 0:L]

        delta = sb("delta", [P, 2, 2, T])
        du = sb("du", [P, 2, 2, T])
        split = sb("split", [NSPLIT, 2, T], BF16)
        tmp = sb("tmp", [P, 2, 2, T])
        high = sb("high", [NSPLIT, T], BF16)
        mid = sb("mid", [NSPLIT, T], BF16)
        rest_ranks = sb("rest_ranks", [NSPLIT + R, T])
        rest, ranks = rest_ranks[0:NSPLIT, :], rest_ranks[:, :]
        H = sb("H", [P, NH, T])
        G = sb("G", [P, NG, T])
        Cs = sb("Cs", [P, NC, T])
        dbu = sb("dbu", [P, ND, T])
        carry = sb("carry", [P, TILES])

        f_bias = dbu.rearrange("p a t -> p (a t)")[:, 0:L // I8]
        row_bias = sb("row_bias", [P, A16])
        stats = sb("stats", [P, NCH, 6])
        gn = sb("gn", [P, 8])
        xn = G[:, 0:2, :]
        diag = dbu[:, :, :].rearrange("p a t -> p (a t)")[:, 0:9 * P].rearrange("p (a t) -> p a t", a=9)
        acc = H[:, 0:4, :].rearrange("p a t -> p (a t)").rearrange("p (b t) -> p b t", b=2)

        w1f, w1g = sb("w1f", [P, P]), sb("w1g", [P, P])
        b1c, w2c, b2c = sb("b1c", [P, 1]), sb("w2c", [P, 1]), sb("b2c", [P, 1])
        own = sb("own", [P, I8])
        w2pick = sb("w2pick", [P, 4, 32])
        before = sb("before", [P, T + 3 * P], BF16)
        rden = sb("rden", [P, 2])
        a_xn, a_g = V[:, 0, 0, :], V[:, 0, 1, :]
        tok = ypad[:, 0, 0:32 * (P + 1)].rearrange("p (j d) -> p j d", j=32)
        flat = [x[:].rearrange("p a b t -> p (a b t)") for x in (tmp, delta)]
        Hf = H[:].rearrange("p a t -> p (a t)")
        tanh = [V[:, 1, i // 2, (i % 2) * PASS:(i % 2) * PASS + PASS] for i in range(4)]
        tanh += [Hf[:, 0:PASS], Hf[:, PASS:2 * PASS]] + flat
        scores = du[:].rearrange("p a b t -> p (a b t)")
        scoresT = G[:].rearrange("p a t -> p (a t)")
        att = Cs[:, 0, 0:P]
        sel = Cs[:, 1:3, :]

        Gf = G[:].rearrange("p a t -> p (a t)")
        used = [0]

        def in_g(*shape):
            n = math.prod(shape)
            v = Gf[:, used[0]:used[0] + n]
            used[0] += n
            return v if len(shape) == 1 else v.rearrange("p (a b) -> p a b", a=shape[0])

        moe = [dict(gw=in_g(E64), gb=in_g(1), b1=in_g(4, E64), b2=in_g(P)) for _ in range(2)]
        wq, wk, wv, qkvb = in_g(P), in_g(P), in_g(P), in_g(3)
        kvs = in_g(NCH + 2)
        top8 = in_g(2, TOP)
        esum = in_g(2, 3)

        s_w = sem("weights_loaded", False)
        s_const = sem("constants_made", False)
        s_aexp = sem("decay_rates_made", False)
        bar = sem("stage_ended", False)
        waits_taken = sem("waits_taken", False)
        s_x = sem("image_loaded", False)
        s_store = sem("result_stored", False)

        b_ready, dbu_done = sem("b_ready"), sem("dbu_done")
        a_ready, scan_done = sem("decay_ready"), sem("scan_done")
        c_psum, c_ready = sem("c_in_psum"), sem("c_ready")
        g_done, ysum_done = sem("g_done"), sem("ysum_done")
        evac = sem("y_added")
        carried = sem("carry_saved")
        xp_done, hi_done, rk_done, rest_done = sem("xproj_done"), sem("high_done"), sem("ranks_done"), sem("rest_done")
        mid_done, split_done = sem("mid_done"), sem("split_done")
        dt0_done, dt1_done = sem("dt0_done"), sem("dt1_done")
        ar0_done, ar1_done = sem("abs_relu0_done"), sem("abs_relu1_done")
        ex_done, lnsq_done, w_done = sem("exp_done"), sem("log_square_done"), sem("small_done")
        mx_done, delta_done, du_done = sem("max_done"), sem("delta_done"), sem("du_done")

        gn_s, gn_p, gn_v, gn_a = sem("gn_dve"), sem("gn_pe"), sem("gn_scale"), sem("gn_act")
        xn_done, pr_done, pad_done = sem("xn_done"), sem("proj_done"), sem("pad_done")
        border = sem("border_done")
        diag_done, cv_done, cvd_done, silu_done = sem("diag_done"), sem("conv_pe"), sem("conv_dve"), sem("silu_done")
        v_done, yi_done = sem("orders_done"), sem("y_started")
        zx, zp, zs = sem("z_norm"), sem("z_proj"), sem("z_silu")
        k_mu, k_yc, k_sq, k_var, k_rs = sem("mu_done"), sem("centred"), sem("squared"), sem("var_done"), sem("rstd")
        k_yn, k_yl, k_yg, k_op, k_res = sem("normed"), sem("affine"), sem("gated"), sem("out_proj"), sem("residual")

        l_mu, l_c, l_sq, l_var, l_rs, l_n = (sem("ln_mean"), sem("ln_centred"), sem("ln_squared"), sem("ln_var"),
                                             sem("ln_rstd"), sem("ln_done"))
        f_ps, f_mul, f_red = sem("f_in_psum"), sem("f_masked"), sem("f_ready")
        g_ps, g_rdy = sem("g_in_psum"), sem("g_copied")
        tk_ps, tk_rdy = sem("tokens_in_psum"), sem("tokens_ready")
        rb_done, th_done, sc_mm = sem("row_bias_ready"), sem("tanh_done"), sem("tanh_group_read")
        e_done, m_done = sem("scores_exp"), sem("scores_masked")
        t_ps, t_sb, o_mm, o_ps = sem("scores_turned"), sem("turned_copied"), sem("turned_read"), sem("attended")
        den_s, att_s, at_ps, at_add = sem("denominator"), sem("attended_scaled"), sem("attended_turned"), sem("attended_added")

        lg_ps, lg_rdy = sem("logits_in_psum"), sem("logits_ready")
        r_max, r_mark, r_neg, r_exp, r_inv, r_w, r_scaled = (sem("top8_found"), sem("top8_marked"), sem("minus_max"),
                                                             sem("logits_exp"), sem("inverse_sum"), sem("routed"), sem("weights_scaled"))
        c_tok_ps, c_w_ps, c_tok, c_w, c_mm, c_out = (sem("block_tokens_psum"), sem("block_weights_psum"), sem("block_tokens"),
                                                     sem("block_weights"), sem("block_pooled"), sem("pooled_copied"))
        d_w1 = [sem(f"w1_loaded{u}", False) for u in range(2)]
        d_w2 = [sem(f"w2_loaded{u}", False) for u in range(2)]
        d_h, d_hb, d_hT, d_o = sem("hidden_in_psum"), sem("hidden_biased"), sem("hidden_ready"), sem("experts_used")
        o_cp, o_t, o_b = sem("out_copied"), sem("out_turned"), sem("out_biased")
        f_ps2, f_add = sem("scattered"), sem("scatter_added")
        q_ps, q_v, q_kv, q_sum, q_out, q_add = (sem("kv_in_psum"), sem("v_ready"), sem("kv_summed"), sem("kv_total"),
                                                sem("q_scaled"), sem("q_added"))
        qq_ps = sem("q_in_psum")

        block = ctx.enter_context(nc.Block())

        def settled(e):
            e.sem_inc(waits_taken, 1)

        def barrier(e, n):
            settled(e)
            e.drain().then_inc(bar, 1)
            e.wait_ge(bar, n * 5 + 5)
            settled(e)

        def at(it, n=0, per=1):
            return it * per + (CR + n + 1)

        def order(k, c):
            if k < 2:
                return V[:, k, :, ds(c * T, T)]
            return V[:, k - 2, :, ds((NCH - 1) * T - c * T, T)]

        def turned(k, v):
            return v if k < 2 else (v[:, :, ::-1] if len(v.shape) == 3 else v[:, ::-1])

        def image(k, c):
            if k % 2 == 0:
                a = c * T if k == 0 else (NCH - 1) * T - c * T
                return Y[:, :, ds(a, T)].rearrange("p s (a b) -> p s a b", a=ROWS)
            a = c * ROWS if k == 1 else W - ROWS - c * ROWS
            return Y.rearrange("p s (h w) -> p s w h", w=W)[:, :, ds(a, ROWS), :]

        def kof(ly, k):
            return k if lay[ly]["kk"] == K else 0

        class Pe:
            def __init__(s, e):
                s.e = e

            def xproj(s, ly, nx):
                k, c, it = nx
                e, w = s.e, lay[ly]
                e.wait_ge(ar1_done, at(it) - 1)
                src = order(0, c) if ly == 0 else order(k, c)
                for h in range(2):
                    m = e.matmul(ps[0:NSPLIT + R, MB, :], w["wx"][:, kof(ly, k), h, :], src[:, h, :],
                                 start=(h == 0), stop=(h == 1))
                m.then_inc(xp_done, 1)

            def dt(s, ly, nx, h):
                k, c, it = nx
                e, w = s.e, lay[ly]
                if h == 0:
                    e.wait_ge(rk_done, at(it))
                    e.wait_ge(rest_done, at(it))
                else:
                    e.wait_ge(ar0_done, at(it))
                e.matmul(ps[:, MB, :], w["wdt"][NSPLIT:, kof(ly, k), h * P:h * P + P], ranks[NSPLIT:, :],
                         start=True, stop=True).then_inc(dt1_done if h else dt0_done, 1)

            def bc(s, it, n, par):
                e = s.e
                if n == 0:
                    e.wait_ge(split_done, at(it))
                e.wait_ge(dbu_done, at(it, 2 * n + 1 - 4, TILES))
                e.matmul(ps[:, B0 + n % 2, :], pick[:, n:n + 1].to_broadcast([NSPLIT, P]), split[:, par, :], start=True, stop=True).then_inc(b_ready, 1)
                e.wait_ge(c_ready, at(it, n - 1, NS))
                e.matmul(ps[:, CB, :], pick[:, NS + n:NS + n + 1].to_broadcast([NSPLIT, P]), split[:, par, :], start=True, stop=True).then_inc(c_psum, 1)

            def ysum(s, it, n):
                e = s.e
                if n == 0:
                    e.wait_ge(evac, at(it) - 1)
                for h in range(2):
                    j = 2 * n + h
                    e.wait_ge(g_done, at(it, j, TILES))
                    e.matmul(ps[:, Y0 + h, :], ident[:, :], G[:, j % NG, :],
                             start=(n == 0), stop=(n == NS - 1)).then_inc(ysum_done, 1)

            def pre(s, ly, nx):
                s.xproj(ly, nx)
                s.dt(ly, nx, 0)
                s.dt(ly, nx, 1)
                s.bc(nx[2], 0, 0)
                s.bc(nx[2], 1, 0)

            def main(s, ly, it, par, nx, prev):
                for n in range(NS):
                    if n < NS - 2:
                        s.bc(it, n + 2, par)
                    elif nx:
                        s.bc(nx[2], n + 2 - NS, 1 - par)
                    s.ysum(it, n)
                    if nx and n == 2:
                        s.xproj(ly, nx)
                    if nx and n in (6, 8):
                        s.dt(ly, nx, (n - 6) // 2)

        class Act:
            def __init__(s, e):
                s.e = e

            def split_high(s, ly, nx):
                e, it = s.e, nx[2]
                bank = turned(nx[0] * ly, ps[0:NSPLIT + R, MB, :])
                e.wait_ge(xp_done, at(it))
                e.activation(high[:, :], bank[0:NSPLIT], ACT.Copy).then_inc(hi_done, 1)
                e.activation(ranks[NSPLIT:, :], bank[NSPLIT:], ACT.Copy).then_inc(rk_done, 1)

            def split_mid(s, nx):
                e, it = s.e, nx[2]
                e.wait_ge(rest_done, at(it))
                e.activation(mid[:, :], rest[:, :], ACT.Copy).then_inc(mid_done, 1)

            def abs_relu(s, ly, nx, h, par):
                e, (k, c, it) = s.e, nx
                bias = lay[ly]["dtb"][:, kof(ly, k), h:h + 1]
                e.wait_ge(dt1_done if h else dt0_done, at(it))
                if h == 0:
                    e.wait_ge(delta_done, at(it) - 1)
                e.activation(tmp[:, 0, h, :], ps[:, MB, :], ACT.Abs, bias=bias)
                e.activation(delta[:, par, h, :], ps[:, MB, :], ACT.Relu, bias=bias).then_inc(ar1_done if h else ar0_done, 1)

            def exp_log(s, nx, par):
                e, it = s.e, nx[2]
                e.wait_ge(ar1_done, at(it))
                e.activation(tmp[:, 0], tmp[:, 0], ACT.Exp, scale=-1.0).then_inc(ex_done, 1)
                e.wait_ge(ex_done, at(it))
                e.activation(tmp[:, 1], tmp[:, 0], ACT.Ln, bias=1.0)
                e.activation(du[:, par], tmp[:, 0], ACT.Square, scale=math.sqrt(0.5)).then_inc(lnsq_done, 1)

            def pre(s, ly, nx):
                s.split_high(ly, nx)
                s.split_mid(nx)
                s.abs_relu(ly, nx, 0, 0)
                s.abs_relu(ly, nx, 1, 0)
                s.exp_log(nx, 0)

            def main(s, ly, it, par, k, nx):
                e, w = s.e, lay[ly]
                for n in range(NS):
                    e.wait_ge(c_psum, at(it, n, NS))
                    e.wait_ge(g_done, at(it, 2 * (n - NC) + 1, TILES))
                    e.activation(Cs[:, n % NC, :], ps[:, CB, :], ACT.Copy).then_inc(c_ready, 1)
                    if n == 0:
                        e.wait_ge(delta_done, at(it))
                    for h in range(2):
                        j = 2 * n + h
                        e.wait_ge(scan_done, at(it, j - 2, TILES))
                        e.activation(ps[:, A0 + j % 2, :], delta[:, par, h, :], ACT.Exp,
                                     scale=w["na"][:, kof(ly, k), h, n:n + 1]).then_inc(a_ready, 1)
                    if nx:
                        if n == 4:
                            s.split_high(ly, nx)
                        if n == 6:
                            s.split_mid(nx)
                        if n in (7, 9):
                            s.abs_relu(ly, nx, (n - 7) // 2, 1 - par)
                        if n == 10:
                            s.exp_log(nx, 1 - par)

        class Dve:
            def __init__(s, e):
                s.e = e

            def split_rest(s, ly, nx):
                e, it = s.e, nx[2]
                e.wait_ge(hi_done, at(it))
                e.wait_ge(mid_done, at(it) - 1)
                e.scalar_tensor_tensor(rest[:, :], high[:, :], keep_mid[:, :],
                                       turned(nx[0] * ly, ps[0:NSPLIT, MB, :]),
                                       ALU.mult, ALU.add).then_inc(rest_done, 1)

            def split_low(s, nx, par):
                e, it = s.e, nx[2]
                e.wait_ge(mid_done, at(it))
                e.scalar_tensor_tensor(split[:, par, :], mid[:, :], keep_low[:, :], rest[:, :],
                                       ALU.mult, ALU.add).then_inc(split_done, 1)

            def softplus_max(s, nx, par):
                e, it = s.e, nx[2]
                e.wait_ge(w_done, at(it))
                e.tensor_tensor(tmp[:, 1], tmp[:, 1], du[:, par], ALU.max).then_inc(mx_done, 1)

            def softplus_add(s, nx, par):
                e, it = s.e, nx[2]
                e.wait_ge(mx_done, at(it))
                e.tensor_tensor(delta[:, par], tmp[:, 1], delta[:, par], ALU.add).then_inc(delta_done, 1)

            def mult(s, it, j, par):
                e = s.e
                n, h = j // 2, j % 2
                if j == 0:
                    e.wait_ge(du_done, at(it))
                if h == 0:
                    e.wait_ge(b_ready, at(it, n, NS))
                e.wait_ge(scan_done, at(it, j - ND, TILES))
                e.tensor_tensor(dbu[:, j % ND, :], du[:, par, h, :], ps[:, B0 + n % 2, :], ALU.mult).then_inc(dbu_done, 1)

            def scan(s, it, j):
                e = s.e
                e.wait_ge(a_ready, at(it, j, TILES))
                e.wait_ge(dbu_done, at(it, j, TILES))
                e.wait_ge(g_done, at(it, j - NH, TILES))
                e.tensor_tensor_scan(H[:, j % NH, :], ps[:, A0 + j % 2, :], dbu[:, j % ND, :], carry[:, j:j + 1],
                                     ALU.mult, ALU.add).then_inc(scan_done, 1)

            def store_states(s, it, g):
                e = s.e
                e.wait_ge(scan_done, at(it, 4 * g + 3, TILES))
                a = (4 * g) % NH
                e.tensor_copy(carry[:, 4 * g:4 * g + 4], H[:, a:a + 4, T - 1]).then_inc(carried, 1)

            def add_y(s, prev):
                e, (k, c, it) = s.e, prev
                e.wait_ge(ysum_done, at(it, TILES - 1, TILES))
                v = image(k, c)
                e.tensor_tensor(v, v, turned(k, ps[:, Y0:Y0 + 2, :]).rearrange("p s (a b) -> p s a b", a=ROWS),
                                ALU.add).then_inc(evac, 1)

            def pre(s, ly, nx):
                s.split_rest(ly, nx)
                s.split_low(nx, 0)
                s.softplus_max(nx, 0)
                s.softplus_add(nx, 0)
                s.e.memset(carry[:, :], 0.0).then_inc(carried, TILES // 4)
                s.mult(nx[2], 0, 0)

            def main(s, ly, it, par, nx, prev, last):
                e = s.e
                for j in range(TILES):
                    if j + 1 < TILES:
                        s.mult(it, j + 1, par)
                    elif nx:
                        s.mult(nx[2], 0, 1 - par)
                    if j == 0:
                        e.wait_ge(carried, at(it, TILES // 4 - 1, TILES // 4))
                    s.scan(it, j)
                    if j % 4 == 0 and j and not last:
                        s.store_states(it, j // 4 - 1)
                    if j == 2 and prev:
                        s.add_y(prev)
                    if nx:
                        if j == 10:
                            s.split_rest(ly, nx)
                        if j == 14:
                            s.split_low(nx, 1 - par)
                        if j == 25:
                            s.softplus_max(nx, 1 - par)
                        if j == 27:
                            s.softplus_add(nx, 1 - par)
                if not last:
                    s.store_states(it, TILES // 4 - 1)
                elif nx:
                    e.wait_ge(scan_done, at(it, TILES - 1, TILES))
                    e.memset(carry[:, :], 0.0).then_inc(carried, TILES // 4)

        class Pool:
            def __init__(s, e):
                s.e = e

            def small(s, nx, par):
                e, it = s.e, nx[2]
                e.wait_ge(lnsq_done, at(it))
                e.tensor_tensor(du[:, par], tmp[:, 0], du[:, par], ALU.subtract).then_inc(w_done, 1)

            def inputs(s, nx, par):
                e, (k, c, it) = s.e, nx
                e.wait_ge(delta_done, at(it))
                e.tensor_tensor(turned(k, du[:, par]), turned(k, delta[:, par]), order(k, c), ALU.mult).then_inc(du_done, 1)

            def pre(s, ly, nx):
                s.small(nx, 0)
                s.inputs(nx, 0)

            def main(s, it, par, nx):
                e = s.e
                for j in range(TILES):
                    n = j // 2
                    if j % 2 == 0:
                        e.wait_ge(c_ready, at(it, n, NS))
                    e.wait_ge(scan_done, at(it, j, TILES))
                    e.wait_ge(ysum_done, at(it, j - NG, TILES))
                    e.tensor_tensor(G[:, j % NG, :], H[:, j % NH, :], Cs[:, n % NC, :], ALU.mult).then_inc(g_done, 1)
                    if nx:
                        if j == 22:
                            s.small(nx, 1 - par)
                        if j == 28:
                            s.inputs(nx, 1 - par)

        def chunks(e, ly, b, run):
            base = b * (2 * K * NCH) + ly * K * NCH
            for k in range(K):
                it = base + k * NCH
                run(k, it, 0, (k, 1, it + 1), (k - 1, NCH - 1, it - 1) if k else None, False)
                settled(e)
                with e.Fori(0, (NCH - 2) // 2) as p:
                    for u in range(2):
                        c = 2 * p + (1 + u)
                        i = it + c
                        run(k, i, 1 - u, (k, c + 1, i + 1), (k, c - 1, i - 1), False)
                i = it + (NCH - 1)
                run(k, i, 1, (k + 1, 0, i + 1) if k + 1 < K else None, (k, NCH - 2, i - 1), True)
            return base

        def first(ly, b):
            return (0, 0, b * (2 * K * NCH) + ly * K * NCH)

        def of(q, n, per):
            return q * per + (CR + n + 1)

        padv = ypad[:, :, :].rearrange("p s (a b) -> p s a b", a=PW)
        CP = 4

        def dve_front(e, ly, q):
            w = lay[ly]
            for c in range(NCH):
                i = e.bn_stats(stats[:, c, :], xT[:, c * T:c * T + T])
            i.then_inc(gn_s, 1)
            e.wait_ge(gn_s, of(q, 0, 3))
            settled(e)
            e.bn_aggr(gn[:, 0:2], stats[:, :, :].rearrange("p a b -> p (a b)")).then_inc(gn_s, 1)
            e.memset(padv[:, :, 0:PW:PW - 1, :], 0.0)
            e.memset(padv[:, :, 1:PW - 1, 0:PW:PW - 1], 0.0).then_inc(border, 1)
            e.wait_ge(gn_p, of(q, 0, 2))
            e.tensor_copy(gn[:, 2:4], ps[:, 0, 0:2]).then_inc(gn_v, 1)
            e.wait_ge(gn_v, of(q, 0, 4))
            e.tensor_tensor(gn[:, 4:5], gn[:, 0:1], gn[:, 2:3], ALU.subtract).then_inc(gn_v, 1)
            e.wait_ge(gn_v, of(q, 1, 4))
            e.tensor_tensor(gn[:, 5:6], gn[:, 4:5], gn[:, 4:5], ALU.mult).then_inc(gn_s, 1)
            e.wait_ge(gn_p, of(q, 1, 2))
            e.tensor_tensor(gn[:, 4:5], gn[:, 3:4], ps[:, 0, 2:3], ALU.add).then_inc(gn_v, 1)
            e.wait_ge(gn_a, of(q, 1, 2))
            e.scalar_tensor_tensor(gn[:, 7:8], gn[:, 2:3], -1.0, gn[:, 6:7], ALU.mult, ALU.mult).then_inc(gn_v, 1)
            for tap in range(9):
                i = e.tensor_scalar(diag[:, tap, :], ident[:, :], w["cw"][:, 0, tap:tap + 1], None, ALU.mult)
            i.then_inc(diag_done, 1)
            e.wait_ge(gn_v, of(q, 3, 4))
            for c in range(NCH):
                if c >= 2:
                    e.wait_ge(pr_done, of(q, 2 * (c - 2) + 1, 2 * NCH))
                e.tensor_scalar(xn[:, c % 2, :], xT[:, c * T:c * T + T], gn[:, 6:7], gn[:, 7:8],
                                ALU.mult, ALU.add).then_inc(xn_done, 1)
            for p in range(CP):
                last = min(2 * p + 2, NCH - 1)
                e.wait_ge(pad_done, of(q, 2 * last + 1, 2 * NCH))
                if p >= 2:
                    e.wait_ge(silu_done, of(q, NCH + p - 2, NCH + CP))
                dst = acc[:, p % 2, :].rearrange("p (a b) -> p a b", a=16)
                for tap in range(9):
                    src = padv[:, 1, 16 * p + tap // 3:16 * p + tap // 3 + 16, tap % 3:tap % 3 + W]
                    if tap == 0:
                        e.tensor_scalar(dst, src, w["cw"][:, 1, 0:1], w["cb"][:, 1:2], ALU.mult, ALU.add).then_inc(cvd_done, 1)
                    else:
                        e.wait_ge(cvd_done, of(q, 9 * p + tap - 1, 9 * CP))
                        e.scalar_tensor_tensor(dst, src, w["cw"][:, 1, tap:tap + 1], dst, ALU.mult, ALU.add).then_inc(cvd_done, 1)
            e.wait_ge(v_done, of(q, 7, 8))
            e.wait_ge(cv_done, of(q, NCH - 1, NCH))
            for h in range(2):
                e.tensor_scalar(Y[:, h, :], V[:, 0, h, :], w["dsum"][:, 0, h:h + 1], None, ALU.mult).then_inc(yi_done, 1)
            for h in range(2):
                e.wait_ge(yi_done, of(q, h, 4))
                yv = Y[:, h, :].rearrange("p (h w) -> p w h", w=W)
                e.scalar_tensor_tensor(yv, V[:, 1, h, :].rearrange("p (w h) -> p w h", w=W), w["dsum"][:, 1, h:h + 1],
                                       yv, ALU.mult, ALU.add).then_inc(yi_done, 1)

        def pe_front(e, ly, q):
            w = lay[ly]
            e.wait_ge(gn_s, of(q, 1, 3))
            e.matmul(ps[:, 0, 0:2], group_mean[:, :], gn[:, 0:2], start=True, stop=True).then_inc(gn_p, 1)
            e.wait_ge(gn_s, of(q, 2, 3))
            e.matmul(ps[:, 0, 2:3], group_mean[:, :], gn[:, 5:6], start=True, stop=True).then_inc(gn_p, 1)
            for c in range(NCH):
                e.wait_ge(xn_done, of(q, c, NCH))
                for h in range(2):
                    if c >= 2:
                        e.wait_ge(pad_done, of(q, 2 * (c - 2) + h, 2 * NCH))
                    e.matmul(ps[:, 2 + 2 * (c % 2) + h, :], w["win"][:, h * P:h * P + P], xn[:, c % 2, :],
                             start=True, stop=True).then_inc(pr_done, 1)
            e.wait_ge(diag_done, of(q, 0, 1))
            for c in range(NCH):
                e.wait_ge(pad_done, of(q, 2 * min(c + 1, NCH - 1), 2 * NCH))
                if c >= 2:
                    e.wait_ge(silu_done, of(q, c - 2, NCH + CP))
                for tap in range(9):
                    a = ROWS * c + tap // 3
                    m = e.matmul(ps[:, 6 + c % 2, :], diag[:, tap, :], padv[:, 0, a:a + ROWS, tap % 3:tap % 3 + W],
                                 start=(tap == 0), stop=(tap == 8))
                m.then_inc(cv_done, 1)

        def act_front(e, ly, q):
            w = lay[ly]
            e.wait_ge(gn_v, of(q, 2, 4))
            e.activation(gn[:, 6:7], gn[:, 4:5], ACT.Ln, bias=eps[:, 0:1]).then_inc(gn_a, 1)
            e.wait_ge(gn_a, of(q, 0, 2))
            e.activation(gn[:, 6:7], gn[:, 6:7], ACT.Exp, scale=-0.5).then_inc(gn_a, 1)
            e.wait_ge(border, of(q, 0, 1))
            for c in range(NCH):
                for h in range(2):
                    e.wait_ge(pr_done, of(q, 2 * c + h, 2 * NCH))
                    e.activation(padv[:, h, 1 + ROWS * c:1 + ROWS * c + ROWS, 1:1 + W],
                                 ps[:, 2 + 2 * (c % 2) + h, :].rearrange("p (a b) -> p a b", a=ROWS),
                                 ACT.Copy).then_inc(pad_done, 1)

            def silu(dst_h, row, rows, src, bias):
                if ly == 0:
                    e.activation(V[:, 0, dst_h, row * W:(row + rows) * W], src, ACT.Silu, bias=bias).then_inc(silu_done, 1)
                else:
                    hg, wh = row // 16, row % 16
                    v = V[:, 0, dst_h, hg * 1024:hg * 1024 + 1024].rearrange("p (g a b) -> p a g b", g=4, a=16)
                    e.activation(v[:, wh:wh + rows], src.rearrange("p (a g b) -> p a g b", a=rows, g=4),
                                 ACT.Silu, bias=bias).then_inc(silu_done, 1)

            for c in range(NCH):
                e.wait_ge(cv_done, of(q, c, NCH))
                silu(0, ROWS * c, ROWS, ps[:, 6 + c % 2, :], w["cb"][:, 0:1])
            for p in range(CP):
                e.wait_ge(cvd_done, of(q, 9 * p + 8, 9 * CP))
                silu(1, 16 * p, 16, acc[:, p % 2, :], 0.0)
            e.wait_ge(silu_done, of(q, NCH + CP - 1, NCH + CP))
            for h in range(2):
                for g in range(4):
                    dst = V[:, 1, h, g * 1024:g * 1024 + 1024]
                    if ly == 0:
                        src = V[:, 0, h, :].rearrange("p (h w) -> p w h", w=W)[:, 16 * g:16 * g + 16, :]
                        dst = dst.rearrange("p (w h) -> p w h", w=16)
                    else:
                        src = V[:, 0, h, :].rearrange("p (a g h w) -> p g a w h", a=4, g=4, h=16)[:, g]
                        dst = dst.rearrange("p (a w h) -> p a w h", a=4, w=16)
                    e.activation(dst, src, ACT.Copy).then_inc(v_done, 1)

        def dve_back(e, ly, q):
            for c in range(NCH):
                if c >= 2:
                    e.wait_ge(zp, of(q, 2 * (c - 2) + 1, 2 * NCH))
                e.tensor_scalar(xn[:, c % 2, :], xT[:, c * T:c * T + T], gn[:, 6:7], gn[:, 7:8],
                                ALU.mult, ALU.add).then_inc(zx, 1)
            yc, yn = delta, du

            def centre(c):
                e.wait_ge(k_mu, of(q, c, NCH))
                if c >= 2:
                    e.wait_ge(k_yn, of(q, 2 * (c - 2) + 1, 2 * NCH))
                for h in range(2):
                    e.tensor_tensor(yc[:, c % 2, h, :], Y[:, h, c * T:c * T + T], ps[:, c % 2, :], ALU.subtract).then_inc(k_yc, 1)

            def norm(c):
                e.wait_ge(k_rs, of(q, 2 * c + 1, 2 * NCH))
                if c >= 2:
                    e.wait_ge(k_op, of(q, c - 2, NCH))
                for h in range(2):
                    e.tensor_tensor(yn[:, c % 2, h, :], yc[:, c % 2, h, :], H[:, c % 2, :], ALU.mult).then_inc(k_yn, 1)

            def gate(c):
                for h in range(2):
                    e.wait_ge(k_yl, of(q, 2 * c + h, 2 * NCH))
                e.tensor_tensor(yn[:, c % 2], yn[:, c % 2], V[:, 0, :, c * T:c * T + T], ALU.mult).then_inc(k_yg, 1)

            def add(c):
                e.wait_ge(k_op, of(q, c, NCH))
                e.tensor_tensor(xT[:, c * T:c * T + T], xT[:, c * T:c * T + T], ps[:, 4 + c % 2, :], ALU.add).then_inc(k_res, 1)

            for i in range(NCH + 3):
                if i < NCH:
                    centre(i)
                if 1 <= i <= NCH:
                    norm(i - 1)
                if 2 <= i <= NCH + 1:
                    gate(i - 2)
                if i >= 3:
                    add(i - 3)

        def pe_back(e, ly, q):
            w = lay[ly]
            for c in range(NCH):
                e.wait_ge(zx, of(q, c, NCH))
                for h in range(2):
                    if c >= 2:
                        e.wait_ge(zs, of(q, 2 * (c - 2) + h, 2 * NCH))
                    e.matmul(ps[:, 2 + 2 * (c % 2) + h, :], w["win"][:, DI + h * P:DI + h * P + P], xn[:, c % 2, :],
                             start=True, stop=True).then_inc(zp, 1)
            for h in range(2):
                e.wait_ge(zs, of(q, 2 * NCH - 1, 2 * NCH))

            def mu(c):
                if c >= 2:
                    e.wait_ge(k_yc, of(q, 2 * (c - 2) + 1, 2 * NCH))
                for h in range(2):
                    m = e.matmul(ps[:, c % 2, :], mean256[:, :], Y[:, h, c * T:c * T + T], start=(h == 0), stop=(h == 1))
                m.then_inc(k_mu, 1)

            def var(c):
                e.wait_ge(k_sq, of(q, c, NCH))
                if c >= 2:
                    e.wait_ge(k_rs, of(q, 2 * (c - 2), 2 * NCH))
                for h in range(2):
                    m = e.matmul(ps[:, 2 + c % 2, :], mean256[:, :], tmp[:, c % 2, h, :], start=(h == 0), stop=(h == 1))
                m.then_inc(k_var, 1)

            def outp(c):
                e.wait_ge(k_yg, of(q, c, NCH))
                if c >= 2:
                    e.wait_ge(k_res, of(q, c - 2, NCH))
                for h in range(2):
                    m = e.matmul(ps[:, 4 + c % 2, :], w["wo"][:, h, :], du[:, c % 2, h, :], start=(h == 0), stop=(h == 1))
                m.then_inc(k_op, 1)

            for i in range(NCH + 3):
                if i < NCH:
                    mu(i)
                if 1 <= i <= NCH:
                    var(i - 1)
                if i >= 3:
                    outp(i - 3)

        def act_back(e, ly, q):
            w = lay[ly]
            for c in range(NCH):
                for h in range(2):
                    e.wait_ge(zp, of(q, 2 * c + h, 2 * NCH))
                    e.activation(V[:, 0, h, c * T:c * T + T], ps[:, 2 + 2 * (c % 2) + h, :], ACT.Silu).then_inc(zs, 1)
            settled(e)
            e.preload_act_table_set("natural_log_exp_and_others")

            def square(c):
                e.wait_ge(k_yc, of(q, 2 * c + 1, 2 * NCH))
                if c >= 2:
                    e.wait_ge(k_var, of(q, c - 2, NCH))
                e.activation(tmp[:, c % 2], delta[:, c % 2], ACT.Square).then_inc(k_sq, 1)

            def rstd(c):
                e.wait_ge(k_var, of(q, c, NCH))
                if c >= 2:
                    e.wait_ge(k_yn, of(q, 2 * (c - 2) + 1, 2 * NCH))
                e.activation(H[:, 2 + c % 2, :], ps[:, 2 + c % 2, :], ACT.Ln, bias=eps[:, 0:1]).then_inc(k_rs, 1)
                e.wait_ge(k_rs, of(q, 2 * c, 2 * NCH))
                e.activation(H[:, c % 2, :], H[:, 2 + c % 2, :], ACT.Exp, scale=-0.5).then_inc(k_rs, 1)

            def affine(c):
                for h in range(2):
                    e.wait_ge(k_yn, of(q, 2 * c + h, 2 * NCH))
                    e.activation(du[:, c % 2, h, :], du[:, c % 2, h, :], ACT.Identity, scale=w["lw"][:, h:h + 1],
                                 bias=w["lb"][:, h:h + 1]).then_inc(k_yl, 1)

            for i in range(NCH + 2):
                if i < NCH:
                    square(i)
                if 1 <= i <= NCH:
                    rstd(i - 1)
                if i >= 2:
                    affine(i - 2)

        def ln_pe(e, q, src):
            def mu(c):
                if c >= 2:
                    e.wait_ge(l_c, of(q, c - 2, NCH))
                e.matmul(ps[:, c % 2, :], mean128[:, :], src(c), start=True, stop=True).then_inc(l_mu, 1)

            def var(c):
                e.wait_ge(l_sq, of(q, c, NCH))
                if c >= 2:
                    e.wait_ge(l_rs, of(q, 2 * (c - 2), 2 * NCH))
                e.matmul(ps[:, 2 + c % 2, :], mean128[:, :], tmp[:, c % 2, 0, :], start=True, stop=True).then_inc(l_var, 1)

            for i in range(NCH + 1):
                if i < NCH:
                    mu(i)
                if i >= 1:
                    var(i - 1)

        def ln_act(e, q, dst):
            for i in range(NCH + 1):
                if i < NCH:
                    e.wait_ge(l_c, of(q, i, NCH))
                    if i >= 2:
                        e.wait_ge(l_var, of(q, i - 2, NCH))
                    e.activation(tmp[:, i % 2, 0, :], dst(i), ACT.Square).then_inc(l_sq, 1)
                if i >= 1:
                    c = i - 1
                    e.wait_ge(l_var, of(q, c, NCH))
                    if c >= 2:
                        e.wait_ge(l_n, of(q, c - 2, NCH))
                    e.activation(H[:, 2 + c % 2, :], ps[:, 2 + c % 2, :], ACT.Ln, bias=eps[:, 0:1]).then_inc(l_rs, 1)
                    e.wait_ge(l_rs, of(q, 2 * c, 2 * NCH))
                    e.activation(H[:, c % 2, :], H[:, 2 + c % 2, :], ACT.Exp, scale=-0.5).then_inc(l_rs, 1)

        def ln_dve(e, q, src, dst):
            for i in range(NCH + 1):
                if i < NCH:
                    e.wait_ge(l_mu, of(q, i, NCH))
                    e.tensor_tensor(dst(i), src(i), ps[:, i % 2, :], ALU.subtract).then_inc(l_c, 1)
                if i >= 1:
                    c = i - 1
                    e.wait_ge(l_rs, of(q, 2 * c + 1, 2 * NCH))
                    e.tensor_tensor(dst(c), dst(c), H[:, c % 2, :], ALU.mult).then_inc(l_n, 1)

        def cols(v):
            return lambda c: v[:, c * T:c * T + T]

        JB = L // T
        passes = [(J, off, min(PASS, J * T - off)) for J in range(1, JB + 1) for off in range(0, J * T, PASS)]
        NP1 = [len([x for x in passes if x[0] == J]) for J in range(1, JB + 1)]
        TOT_P = 4 * sum(NP1)
        TOT_B = 4 * sum(J * 4 for J in range(1, JB + 1)) // 4

        def walk(e, b, run):
            np_, nb_ = 0, 0
            for J in range(1, JB + 1):
                mine = [x for x in passes if x[0] == J]
                settled(e)
                with e.Fori(0, 4) as r:
                    p0 = b * TOT_P + (r * len(mine) + np_)
                    b0 = b * TOT_B + (r * J + nb_)
                    run(J, r, b * 32 + (r + 4 * (J - 1)), [(off, N, p0 + i, b0 + off // T) for i, (_, off, N) in enumerate(mine)])
                np_ += 4 * len(mine)
                nb_ += 4 * J

        def val(i, per=1, n=0):
            return i * per + (CR + n + 1)

        def pe_attn(e, b):
            ln_pe(e, b, cols(xT))
            for c in range(NCH):
                e.wait_ge(l_n, of(b, c, NCH))
                if c >= 2:
                    e.wait_ge(f_mul, of(b, c - 2, NCH))
                e.matmul(ps[:, 4 + c % 2, :], w1f[:, :], a_xn[:, c * T:c * T + T], start=True, stop=True).then_inc(f_ps, 1)
                if c >= 2:
                    e.wait_ge(g_rdy, of(b, c - 2, NCH))
                e.matmul(ps[:, 6 + c % 2, :], w1g[:, :], a_xn[:, c * T:c * T + T], start=True, stop=True).then_inc(g_ps, 1)
            e.wait_ge(l_rs, of(b, 2 * NCH - 1, 2 * NCH))
            for c in range(NCH):
                if c >= 2:
                    e.wait_ge(tk_rdy, of(b, c - 2, NCH))
                for i in range(4):
                    a = c * T + i * P
                    m = e.transpose(ps[:, c % 2, i * P:i * P + P], a_xn[:, a:a + P], ident[:, :])
                m.then_inc(tk_ps, 1)
            e.wait_ge(tk_rdy, of(b, NCH - 1, NCH))
            e.wait_ge(f_red, of(b, NCH - 1, NCH))
            e.wait_ge(g_rdy, of(b, NCH - 1, NCH))

            def block_(J, r, blk, mine):
                for i, (off, N, p, bank) in enumerate(mine):
                    e.wait_ge(e_done, val(p) - 1)
                    for u in range(4):
                        e.wait_ge(th_done, val(p, 16, 4 * u + 3))
                        for x in range(N // T):
                            for c in range(4):
                                m = e.matmul(ps[32 * c:32 * c + 32, x, :], w2pick[:, u, :],
                                             tanh[(4 * u + c) % NT][:, x * T:x * T + T], start=(u == 0), stop=(u == 3))
                        m.then_inc(sc_mm, 1)
                    e.wait_ge(m_done, val(p))
                    for x in range(N // T):
                        e.wait_ge(t_sb, val(bank + x) - (2 if off + x else 1))
                        for y in range(4):
                            a = x * T + y * P
                            m = e.transpose(ps[:, 4 + (off // T + x) % 2, y * P:y * P + P], scores[:, a:a + P], ident[:, :])
                        m.then_inc(t_ps, 1)
                        if x >= 1:
                            attend(J, blk, off // T + x - 1, bank + x - 1)
                    attend(J, blk, off // T + N // T - 1, bank + N // T - 1)
                e.wait_ge(att_s, val(blk))
                e.transpose(ps[:, 7, 0:P], att, ident[:, :]).then_inc(at_ps, 1)

            def attend(J, blk, x, bank):
                e.wait_ge(t_sb, val(bank))
                if x == 0:
                    e.wait_ge(att_s, val(blk) - 1)
                for y in range(4):
                    m = e.matmul(ps[:, 6, 0:P + 1], scoresT[:, (x % 4) * T + y * P:(x % 4) * T + y * P + P],
                                 tok[:, 4 * x + y, :], start=(x == 0 and y == 0), stop=(x == J - 1 and y == 3))
                m.then_inc(o_mm, 1)
            walk(e, b, block_)

        def act_attn(e, b):
            ln_act(e, b, cols(a_xn))
            for c in range(NCH):
                e.wait_ge(g_ps, of(b, c, NCH))
                e.activation(a_g[:, c * T:c * T + T], ps[:, 6 + c % 2, :], ACT.Identity, bias=b1c[:, :]).then_inc(g_rdy, 1)
            for c in range(NCH):
                e.wait_ge(tk_ps, of(b, c, NCH))
                e.activation(tok[:, 4 * c:4 * c + 4, 0:P], ps[:, c % 2, :].rearrange("p (a d) -> p a d", a=4),
                             ACT.Copy).then_inc(tk_rdy, 1)
            settled(e)
            e.preload_act_table_set("exp_and_others")
            e.wait_ge(g_rdy, of(b, NCH - 1, NCH))
            e.wait_ge(f_red, of(b, NCH - 1, NCH))

            def block_(J, r, blk, mine):
                e.activation(row_bias[:, :], f_bias[:, ds(r * A16 + (J - 1) * 64, A16)], ACT.Copy).then_inc(rb_done, 1)
                e.wait_ge(rb_done, val(blk))
                for i, (off, N, p, bank) in enumerate(mine):
                    for u in range(4):
                        e.wait_ge(sc_mm, val(p, 4, u) - 2)
                        for c in range(4):
                            e.activation(tanh[(4 * u + c) % NT][:, 0:N], a_g[:, off:off + N], ACT.Tanh,
                                         bias=row_bias[:, 4 * c + u:4 * c + u + 1]).then_inc(th_done, 1)
                    e.wait_ge(sc_mm, val(p, 4, 3))
                    e.wait_ge(t_ps, val(bank) - 1)
                    e.activation(scores[:, 0:N], ps[:, 0:N // T, :].rearrange("p a t -> p (a t)"), ACT.Exp,
                                 bias=b2c[:, :]).then_inc(e_done, 1)

            walk(e, b, block_)

        def dve_attn(e, b):
            ln_dve(e, b, cols(xT), cols(a_xn))
            e.memset(tok[:, :, P:P + 1], 1.0)
            for c in range(NCH):
                e.wait_ge(f_ps, of(b, c, NCH))
                if c >= 2:
                    e.wait_ge(f_red, of(b, c - 2, NCH))
                e.tensor_tensor(sel[:, c % 2, :].rearrange("p (a s) -> p a s", s=I8),
                                ps[:, 4 + c % 2, :].rearrange("p (a s) -> p a s", s=I8),
                                own[:, :].rearrange("p (o s) -> p o s", o=1).to_broadcast([P, T // I8, I8]), ALU.mult).then_inc(f_mul, 1)
                e.wait_ge(f_mul, of(b, c, NCH))
                e.reduce_sum(f_bias[:, c * (T // I8):(c + 1) * (T // I8)], sel[:, c % 2, :].rearrange("p (a s) -> p a s", s=I8),
                             axis=mybir.AxisListType.X).then_inc(f_red, 1)

            def block_(J, r, blk, mine):
                for i, (off, N, p, bank) in enumerate(mine):
                    for x in range(N // T):
                        e.wait_ge(t_ps, val(bank + x))
                        e.wait_ge(o_mm, val(bank + x) - 4)
                        y = off // T + x
                        e.tensor_copy(scoresT[:, (y % 4) * T:(y % 4) * T + T], ps[:, 4 + y % 2, :]).then_inc(t_sb, 1)
                e.wait_ge(o_mm, val(mine[-1][3] + (mine[-1][1] // T - 1)))
                e.wait_ge(at_add, val(blk) - 1)
                e.tensor_scalar(rden[:, 0:1], ps[:, 6, P:P + 1], 1e-10, None, ALU.add).then_inc(den_s, 1)
                e.wait_ge(den_s, val(blk, 2, 0))
                e.reciprocal(rden[:, 1:2], rden[:, 0:1]).then_inc(den_s, 1)
                e.wait_ge(den_s, val(blk, 2, 1))
                e.tensor_scalar(att, ps[:, 6, 0:P], rden[:, 1:2], None, ALU.mult).then_inc(att_s, 1)
                e.wait_ge(at_ps, val(blk))
                xb = xT[:, ds(r * P + (J - 1) * T, P)]
                e.tensor_tensor(xb, xb, ps[:, 7, 0:P], ALU.add).then_inc(at_add, 1)

            walk(e, b, block_)

        def pool_attn(e, b):
            def block_(J, r, blk, mine):
                for i, (off, N, p, bank) in enumerate(mine):
                    e.wait_ge(e_done, val(p))
                    if i == len(mine) - 1:
                        d = scores[:, N - T:N]
                        e.tensor_tensor(d, d, before[:, ds(3 * P - r * P, T)], ALU.mult).then_inc(m_done, 1)
                    else:
                        e.nop().then_inc(m_done, 1)

            walk(e, b, block_)

        B = batches
        logit = Y
        work = xT[:, :]
        df = dbu[:].rearrange("p a t -> p (a t)")
        pooled = df[:, 0:4 * E64].rearrange("p (b e) -> p b e", b=4)
        hid = [df[:, T + 128 * u:T + 128 * u + 64] for u in range(2)]
        hidT = [df[:, T + 128 * u + 64:T + 128 * u + 128] for u in range(2)]
        eout = df[:, 2 * T:2 * T + 2 * P].rearrange("p (a o) -> p a o", a=2)
        outT = df[:, 3 * T:3 * T + 4 * E64].rearrange("p (b e) -> p b e", b=4)
        slots = [Hf[:, 0:4 * T], Hf[:, 4 * T:8 * T], flat[1], scores]
        NGRP = E64 // EG

        def img(b):
            return V[:, b // 2, b % 2, :]

        def rows(pair):
            return E64 * min(2, B - 2 * pair)

        def w1s(u):
            return slots[2 * u].rearrange("p (e m c) -> p e m c", e=EG, c=4)

        def w2s(u):
            return slots[2 * u + 1].rearrange("p (e c o) -> p e c o", e=EG, c=4)

        def ehid(v):
            return v[:, 0:EG * 4 * B].rearrange("p (e c b) -> p e c b", e=EG, c=4)

        class PeTail:
            def norm(s, e, q, b):
                ln_pe(e, q, cols(xT))

            def logits(s, e, f):
                for b in range(B):
                    for c in range(NCH):
                        i = (f * B + b) * NCH + c
                        e.wait_ge(lg_rdy, val(i) - 2)
                        e.matmul(ps[E64 * (b % 2):E64 * (b % 2) + E64, c % 2, :], moe[f]["gw"], cols(img(b))(c),
                                 start=True, stop=True).then_inc(lg_ps, 1)

            def route(s, e, f):
                pass

            def pool(s, e, f):
                def turn(sb):
                    i = f * 32 + sb
                    e.wait_ge(c_tok, val(i) - 2)
                    for b in range(B):
                        m = e.transpose(ps[:, 4 + sb % 2, b * P:b * P + P], img(b)[:, sb * P:sb * P + P], ident[:, :])
                    m.then_inc(c_tok_ps, 1)
                    e.wait_ge(c_w, val(i) - 2)
                    for p in range((B + 1) // 2):
                        n = rows(p)
                        m = e.transpose(ps[:, 6 + sb % 2, p * P:p * P + n], logit[0:n, p, sb * P:sb * P + P], ident[0:n, 0:n])
                    m.then_inc(c_w_ps, 1)

                for sb in range(33):
                    if sb < 32:
                        turn(sb)
                    if sb == 0:
                        continue
                    x = sb - 1
                    e.wait_ge(c_tok, val(f * 32 + x))
                    e.wait_ge(c_w, val(f * 32 + x))
                    for b in range(B):
                        a = b * E64
                        m = e.matmul(ps[:, b, 0:E64], Cs[:, x % 2, b * P:b * P + P], Cs[:, 2 + x % 2, a:a + E64],
                                     start=(x == 0), stop=(x == 31))
                    m.then_inc(c_mm, 1)

            def experts(s, e, f):
                def hidden(x2, u):
                    g = 2 * x2 + u
                    i = g + f * NGRP
                    e.wait_ge(d_w1[u], x2 * 16 + (f * NGRP // 2 + 1) * 16)
                    e.wait_ge(d_hb, val(i) - 2)
                    o = ehid(ps[:, 4 + u, :])
                    for x in range(EG):
                        for c in range(4):
                            m = e.matmul(o[:, x, c, :], w1s(u)[:, x, :, c], pooled[:, 0:B, ds(EG * g + x, 1)],
                                         start=True, stop=True)
                    m.then_inc(d_h, 1)

                def output(x2, u):
                    g = 2 * x2 + u
                    i = g + f * NGRP
                    e.wait_ge(d_w2[u], x2 * 16 + (f * NGRP // 2 + 1) * 16)
                    e.wait_ge(d_hT, val(i))
                    for x in range(EG):
                        for c in range(4):
                            m = e.matmul(ps[:, 6, ds((EG * g + x) * B, B)], w2s(u)[:, x, c, :], ehid(hidT[u])[:, x, c, :],
                                         start=(c == 0), stop=(c == 3))
                    m.then_inc(d_o, 1)

                hidden(0, 0)
                with e.Fori(0, NGRP // 2 - 1) as i:
                    hidden(i, 1)
                    output(i, 0)
                    hidden(i + 1, 0)
                    output(i, 1)
                hidden(NGRP // 2 - 1, 1)
                output(NGRP // 2 - 1, 0)
                output(NGRP // 2 - 1, 1)

            def outputs(s, e, f):
                e.wait_ge(o_cp, val(f))
                for p in range((B + 1) // 2):
                    m = e.transpose(ps[0:rows(p), p, 0:P], outT[:, 2 * p:2 * p + rows(p) // E64, :].rearrange("p b e -> p (b e)"),
                                    ident[:, :])
                m.then_inc(o_t, 1)

            def scatter(s, e, f, b):
                a = E64 * (b % 2)
                for c in range(NCH):
                    i = (f * B + b) * NCH + c
                    e.wait_ge(f_add, val(i) - 2)
                    e.matmul(ps[:, 4 + c % 2, :], eout[a:a + E64, b // 2, :], logit[a:a + E64, b // 2, c * T:c * T + T],
                             start=True, stop=True).then_inc(f_ps2, 1)

            def attend(s, e, b):
                for c in range(NCH):
                    i = b * NCH + c
                    e.wait_ge(q_kv, val(i) - 2)
                    e.matmul(ps[:, 4 + c % 2, :], wk, cols(img(b))(c), start=True, stop=True)
                    e.matmul(ps[:, 6 + c % 2, :], wv, cols(img(b))(c), start=True, stop=True).then_inc(q_ps, 1)
                for c in range(NCH):
                    i = b * NCH + c
                    e.wait_ge(q_out, val(i) - 2)
                    e.matmul(ps[:, c % 2, :], wq, cols(img(b))(c), start=True, stop=True).then_inc(qq_ps, 1)

        class ActTail:
            def norm(s, e, q, b):
                ln_act(e, q, cols(img(b)))

            def logits(s, e, f):
                for b in range(B):
                    for c in range(NCH):
                        i = (f * B + b) * NCH + c
                        a = E64 * (b % 2)
                        e.wait_ge(lg_ps, val(i))
                        e.activation(logit[a:a + E64, b // 2, c * T:c * T + T], ps[a:a + E64, c % 2, :], ACT.Identity,
                                     bias=moe[f]["gb"][a:a + E64, :]).then_inc(lg_rdy, 1)

            def route(s, e, f):
                for p in range((B + 1) // 2):
                    n, i = rows(p), f * ((B + 1) // 2) + p
                    e.wait_ge(r_neg, val(i))
                    e.wait_ge(r_mark, val(i))
                    e.activation(logit[0:n, p, :], logit[0:n, p, :], ACT.Exp, bias=esum[0:n, p, 0:1],
                                 accum_out=esum[0:n, p, 1:2]).then_inc(r_exp, 1)

            def pool(s, e, f):
                for sb in range(32):
                    e.wait_ge(c_w_ps, val(f * 32 + sb))
                    if sb >= 2:
                        e.wait_ge(c_mm, val(f * 32 + sb) - 2)
                    e.activation(Cs[:, 2 + sb % 2, 0:E64 * B], ps[:, 6 + sb % 2, 0:E64 * B], ACT.Copy).then_inc(c_w, 1)

            def experts(s, e, f):
                settled(e)
                e.preload_act_table_set("gelu_and_others")

                def act(g, u):
                    i = g + f * NGRP
                    e.wait_ge(d_hb, val(i))
                    e.wait_ge(d_o, val(i) - 2)
                    e.activation(hidT[u][:, 0:EG * 4 * B], hid[u][:, 0:EG * 4 * B], ACT.Gelu).then_inc(d_hT, 1)

                with e.Fori(0, NGRP // 2) as i:
                    act(2 * i, 0)
                    act(2 * i + 1, 1)
                settled(e)
                e.preload_act_table_set("natural_log_exp_and_others")

            def outputs(s, e, f):
                pass

            def scatter(s, e, f, b):
                pass

            def attend(s, e, b):
                for c in range(NCH):
                    e.wait_ge(q_ps, val(b * NCH + c))
                    e.wait_ge(q_kv, val(b * NCH + c) - 2)
                    e.activation(tmp[:, c % 2, 1, :], ps[:, 6 + c % 2, :], ACT.Identity, bias=qkvb[:, 2:3]).then_inc(q_v, 1)
                e.wait_ge(q_sum, val(b, 2, 1))
                for c in range(NCH):
                    e.wait_ge(qq_ps, val(b * NCH + c))
                    if c >= 2:
                        e.wait_ge(q_add, val(b * NCH + c) - 2)
                    e.activation(tmp[:, c % 2, 1, :], ps[:, c % 2, :], ACT.Identity, scale=kvs[:, NCH:NCH + 1],
                                 bias=kvs[:, NCH + 1:NCH + 2]).then_inc(q_out, 1)

        class DveTail:
            def norm(s, e, q, b):
                ln_dve(e, q, cols(xT), cols(img(b)))

            def logits(s, e, f):
                pass

            def route(s, e, f):
                for p in range((B + 1) // 2):
                    n, i = rows(p), f * ((B + 1) // 2) + p
                    x = logit[0:n, p, :]
                    e.max(top8[0:n, p, :], x).then_inc(r_max, 1)
                    e.wait_ge(r_max, val(i))
                    if p:
                        e.wait_ge(r_w, val(i) - 1)
                    e.tensor_scalar(esum[0:n, p, 0:1], top8[0:n, p, 0:1], -1.0, None, ALU.mult).then_inc(r_neg, 1)
                    e.match_replace(work[0:n, :], top8[0:n, p, :], x, LOWEST).then_inc(r_mark, 1)
                    e.wait_ge(r_mark, val(i))
                    e.wait_ge(r_exp, val(i))
                    e.reciprocal(esum[0:n, p, 2:3], esum[0:n, p, 1:2]).then_inc(r_inv, 1)
                    e.scalar_tensor_tensor(x, work[0:n, :], LOWEST, x, ALU.is_le, ALU.mult).then_inc(r_w, 1)
                    e.wait_ge(r_inv, val(i))
                    e.wait_ge(r_w, val(i))
                    e.tensor_scalar(x, x, esum[0:n, p, 2:3], None, ALU.mult).then_inc(r_scaled, 1)

            def pool(s, e, f):
                for sb in range(32):
                    e.wait_ge(c_tok_ps, val(f * 32 + sb))
                    if sb >= 2:
                        e.wait_ge(c_mm, val(f * 32 + sb) - 2)
                    e.tensor_copy(Cs[:, sb % 2, 0:P * B], ps[:, 4 + sb % 2, 0:P * B]).then_inc(c_tok, 1)
                e.wait_ge(c_mm, val(f * 32 + 31))
                e.tensor_copy(pooled[:, 0:B, :], ps[:, 0:B, 0:E64]).then_inc(c_out, 1)

            def experts(s, e, f):
                def bias(g, u):
                    i = g + f * NGRP
                    e.wait_ge(d_h, val(i))
                    e.wait_ge(d_hT, val(i) - 2)
                    b1 = moe[f]["b1"][:, :, ds(EG * g, EG)].rearrange("p c (e o) -> p e c o", o=1)
                    e.tensor_tensor(ehid(hid[u]), ehid(ps[:, 4 + u, :]), b1.to_broadcast([P, EG, 4, B]), ALU.add).then_inc(d_hb, 1)

                with e.Fori(0, NGRP // 2) as i:
                    bias(2 * i, 0)
                    bias(2 * i + 1, 1)

            def outputs(s, e, f):
                e.tensor_copy(outT[:, 0:B, :], ps[:, 6, 0:E64 * B].rearrange("p (e b) -> p b e", b=B)).then_inc(o_cp, 1)
                e.wait_ge(o_t, val(f))
                for p in range((B + 1) // 2):
                    n = rows(p)
                    e.tensor_tensor(eout[0:n, p, :], ps[0:n, p, 0:P], moe[f]["b2"][0:n, :], ALU.add).then_inc(o_b, 1)

            def scatter(s, e, f, b):
                for c in range(NCH):
                    x = cols(xT)(c)
                    e.wait_ge(f_ps2, val((f * B + b) * NCH + c))
                    e.tensor_tensor(x, x, ps[:, 4 + c % 2, :], ALU.add).then_inc(f_add, 1)

            def attend(s, e, b):
                for c in range(NCH):
                    i = b * NCH + c
                    e.wait_ge(q_v, val(i))
                    v = tmp[:, c % 2, 1, :]
                    e.scalar_tensor_tensor(v, ps[:, 4 + c % 2, :], qkvb[:, 1:2], v, ALU.add, ALU.mult,
                                           accum_out=kvs[:, c:c + 1]).then_inc(q_kv, 1)
                e.wait_ge(q_kv, val(b * NCH + NCH - 1))
                e.reduce_sum(kvs[:, NCH:NCH + 1], kvs[:, 0:NCH], axis=mybir.AxisListType.X).then_inc(q_sum, 1)
                e.wait_ge(q_sum, val(b, 2, 0))
                e.tensor_tensor(kvs[:, NCH + 1:NCH + 2], kvs[:, NCH:NCH + 1], qkvb[:, 0:1], ALU.mult).then_inc(q_sum, 1)
                for c in range(NCH):
                    e.wait_ge(q_out, val(b * NCH + c))
                    x = cols(xT)(c)
                    e.tensor_tensor(x, x, tmp[:, c % 2, 1, :], ALU.add).then_inc(q_add, 1)

        class PoolTail:
            def norm(s, e, q, b):
                pass

            logits = route = pool = experts = outputs = lambda s, e, f: None

            def scatter(s, e, f, b):
                pass

            def attend(s, e, b):
                pass

        class SyncTail(PoolTail):
            def experts(s, e, f):
                m = f + 2

                def load(g, u):
                    i = g + f * NGRP
                    e.wait_ge(d_o, val(i) - 2)
                    e.dma_start(slots[2 * u].rearrange("p (e h) -> p e h", e=EG),
                                t[f"u1_{m}"][ds(EG * g, EG), 0:P, :].rearrange("e d h -> d e h")).then_inc(d_w1[u], 16)
                    e.dma_start(slots[2 * u + 1].rearrange("p (e h) -> p e h", e=EG),
                                t[f"u2_{m}"][ds(EG * g, EG), 0:HID, :].rearrange("e (p c) o -> p e (c o)", c=4)).then_inc(d_w2[u], 16)

                with e.Fori(0, NGRP // 2) as i:
                    load(2 * i, 0)
                    load(2 * i + 1, 1)

        def tail(e, x, load, store):
            n = [B * (NSTG + 2)]

            def end():
                barrier(e, n[0])
                n[0] += 1

            load("weights", 0)
            for b in range(B):
                load("x", b)
                end()
                x.norm(e, B + b, b)
                end()
            for f in range(2):
                x.logits(e, f)
                end()
                x.route(e, f)
                end()
                x.pool(e, f)
                end()
                x.experts(e, f)
                end()
                x.outputs(e, f)
                end()
                for b in range(B):
                    load("x", b)
                    end()
                    x.scatter(e, f, b)
                    end()
                    if f == 0:
                        x.norm(e, 2 * B + 2 * b, b)
                        end()
                        x.attend(e, b)
                        end()
                        store(res, b)
                        x.norm(e, 2 * B + 2 * b + 1, b)
                        end()
                    else:
                        store(out, b)
                        end()

        NSTG = 7

        @block.sync
        def _(e):
            n = 0
            for ly, w in enumerate(lay):
                for name in ("win", "cw", "cb", "dtb", "al", "dd", "lw", "lb", "wo"):
                    e.dma_start(w[name][:], t[f"{name}{ly}"]).then_inc(s_w, 16)
                    n += 1
                for i in range(3):
                    e.dma_start(w["wx"][:, :, :, 32 * i:32 * i + 32], t[f"wx{ly}"][:, :, :, R:]).then_inc(s_w, 16)
                e.dma_start(w["wx"][:, :, :, NSPLIT:], t[f"wx{ly}"][:, :, :, 0:R]).then_inc(s_w, 16)
                e.dma_start(w["wdt"][NSPLIT:], t[f"wdt{ly}"]).then_inc(s_w, 16)
                n += 5
            for dst, name in ((w1f, "w1f"), (w1g, "w1g"), (b1c, "b1c"), (w2c, "w2c"), (b2c, "b2c")):
                e.dma_start(dst[:], t[name]).then_inc(s_w, 16)
                n += 1
            assert n == N_WEIGHTS
            with e.Fori(0, batches) as b:
                e.dma_start(xT[:], t["xT"][ds(b, 1)].rearrange("a p l -> (a p) l")).then_inc(s_x, 16)
                e.wait_ge(s_x, b * 16 + 16)
                settled(e)
                barrier(e, b * (NSTG + 2))
                for ly in range(2):
                    for i in range(3):
                        barrier(e, b * (NSTG + 2) + (1 + 3 * ly + i))
                barrier(e, b * (NSTG + 2) + NSTG)
                e.dma_start(res[ds(b, 1)].rearrange("a p l -> (a p) l"), xT[:]).then_inc(s_store, 16)
                e.wait_ge(s_store, b * 16 + 16)
                settled(e)
                barrier(e, b * (NSTG + 2) + (NSTG + 1))

            loads = [B * 16]

            def load(what, b):
                if what == "weights":
                    for dst, name in ((wq, "wq"), (wk, "wk"), (wv, "wv"), (qkvb, "qkvb")):
                        e.dma_start(dst, t[name]).then_inc(s_w, 16)
                    for m, w in zip((2, 3), moe):
                        for name in ("gw", "gb", "b1", "b2"):
                            e.dma_start(w[name], t[f"{name}_{m}"]).then_inc(s_w, 16)
                    e.wait_ge(s_w, 16 * (N_WEIGHTS + 12))
                else:
                    e.dma_start(xT[:], res[b]).then_inc(s_x, 16)
                    loads[0] += 16
                    e.wait_ge(s_x, loads[0])

            stored = [B * 16]

            def store(dst, b):
                e.dma_start(dst[b], xT[:]).then_inc(s_store, 16)
                stored[0] += 16
                e.wait_ge(s_store, stored[0])

            tail(e, SyncTail(), load, store)

        @block.gpsimd
        def _(e):
            e.memset(ident[:], 0.0).then_inc(s_const, 1)
            e.memset(group_mean[:], 0.25).then_inc(s_const, 1)
            e.memset(mean256[:], 1.0 / DI)
            e.memset(mean128[:], 1.0 / P)
            e.memset(pick[:], 0.0).then_inc(s_const, 1)
            e.memset(keep_mid[:], -1.0)
            e.memset(keep_low[:], -1.0).then_inc(s_const, 1)
            e.memset(eps[:, 0:1], 1e-5).then_inc(s_const, 1)
            e.memset(eps[:, 1:2], 1e-10).then_inc(s_const, 1)
            e.memset(before[:], 1.0)
            e.memset(own[:], 1.0)
            e.memset(w2pick[:], 0.0).then_inc(s_const, 1)
            for s in counting:
                e.nop().then_inc(s, CR)
            e.wait_ge(s_const, 7)
            e.affine_select(out=ident[:], in_=ident[:], compare_op=ALU.not_equal, fill=1.0, base=0,
                            pattern=[[-1, P]], channel_multiplier=1).then_inc(s_const, 1)
            gm = group_mean[:].rearrange("p (g m) -> p g m", m=4)
            e.affine_select(out=gm, in_=gm, compare_op=ALU.is_ge, fill=0.0, base=0,
                            pattern=[[-4, 32], [0, 4]], channel_multiplier=1).then_inc(s_const, 1)
            e.affine_select(out=keep_mid[:], in_=keep_mid[:], compare_op=ALU.is_ge, fill=0.0, base=-32,
                            pattern=[[0, 1]], channel_multiplier=1)
            e.affine_select(out=keep_low[:], in_=keep_low[:], compare_op=ALU.is_ge, fill=0.0, base=-64,
                            pattern=[[0, 1]], channel_multiplier=1).then_inc(s_const, 1)
            e.affine_select(out=own[:], in_=own[:], compare_op=ALU.is_ge, fill=0.0, base=0,
                            pattern=[[-A16, I8]], channel_multiplier=1).then_inc(s_const, 1)
            e.affine_select(out=before[:], in_=before[:], compare_op=ALU.is_gt, fill=0.0, base=3 * P,
                            pattern=[[-1, T + 3 * P]], channel_multiplier=1).then_inc(s_const, 1)
            e.wait_ge(s_const, 12)
            e.affine_select(out=own[:], in_=own[:], compare_op=ALU.is_ge, fill=0.0, base=A16 - 1,
                            pattern=[[A16, I8]], channel_multiplier=-1).then_inc(s_const, 1)
            e.affine_select(out=gm, in_=gm, compare_op=ALU.is_ge, fill=0.0, base=3,
                            pattern=[[4, 32], [0, 4]], channel_multiplier=-1).then_inc(s_const, 1)
            for i in range(3):
                e.affine_select(out=pick[:], in_=pick[:], compare_op=ALU.not_equal, fill=1.0, base=-32 * i,
                                pattern=[[-1, 32]], channel_multiplier=1).then_inc(s_const, 1)
                e.wait_ge(s_const, 15 + i)
            x = Pool(e)
            with e.Fori(0, batches) as b:
                barrier(e, b * (NSTG + 2))
                for ly in range(2):
                    barrier(e, b * (NSTG + 2) + (1 + 3 * ly))
                    x.pre(ly, first(ly, b))
                    chunks(e, ly, b, lambda k, it, par, nx, prev, last: x.main(it, par, nx))
                    barrier(e, b * (NSTG + 2) + (2 + 3 * ly))
                    barrier(e, b * (NSTG + 2) + (3 + 3 * ly))
                pool_attn(e, b)
                barrier(e, b * (NSTG + 2) + NSTG)
                barrier(e, b * (NSTG + 2) + (NSTG + 1))
            tail(e, PoolTail(), lambda *a: None, lambda *a: None)

        @block.vector
        def _(e):
            e.wait_ge(s_w, 16 * N_WEIGHTS)
            for ly, w in enumerate(lay):
                e.tensor_scalar(w["al"][:], w["al"][:], 85.0, None, ALU.min).then_inc(s_aexp, 1)
                kk = w["kk"]
                for d in range(2):
                    i = e.tensor_tensor(w["dsum"][:, d, :], w["dd"][:, d % kk, :], w["dd"][:, (d + 2) % kk, :], ALU.add)
                i.then_inc(s_aexp, 1)
            e.wait_ge(s_const, 17)
            for u in range(4):
                e.tensor_scalar(w2pick[:, u, 8 * u:8 * u + 8], own[:, :], w2c[:, :], None, ALU.mult)
            e.wait_ge(s_aexp, 6)
            for ly, w in enumerate(lay):
                e.tensor_scalar(w["na"][:], w["na"][:], -1.0, None, ALU.mult).then_inc(s_aexp, 1)
            x = Dve(e)
            with e.Fori(0, batches) as b:
                barrier(e, b * (NSTG + 2))
                for ly in range(2):
                    dve_front(e, ly, b * 2 + ly)
                    barrier(e, b * (NSTG + 2) + (1 + 3 * ly))
                    x.pre(ly, first(ly, b))
                    base = chunks(e, ly, b, lambda k, it, par, nx, prev, last: x.main(ly, it, par, nx, prev, last))
                    x.add_y((K - 1, NCH - 1, base + (K * NCH - 1)))
                    barrier(e, b * (NSTG + 2) + (2 + 3 * ly))
                    dve_back(e, ly, b * 2 + ly)
                    barrier(e, b * (NSTG + 2) + (3 + 3 * ly))
                dve_attn(e, b)
                barrier(e, b * (NSTG + 2) + NSTG)
                barrier(e, b * (NSTG + 2) + (NSTG + 1))
            tail(e, DveTail(), lambda *a: None, lambda *a: None)

        @block.scalar
        def _(e):
            settled(e)
            e.preload_act_table_set("natural_log_exp_and_others")
            e.wait_ge(s_aexp, 4)
            for ly, w in enumerate(lay):
                e.activation(w["na"][:], w["al"][:], ACT.Exp).then_inc(s_aexp, 1)
            x = Act(e)
            with e.Fori(0, batches) as b:
                barrier(e, b * (NSTG + 2))
                for ly in range(2):
                    act_front(e, ly, b * 2 + ly)
                    settled(e)
                    e.preload_act_table_set("natural_log_exp_and_others")
                    barrier(e, b * (NSTG + 2) + (1 + 3 * ly))
                    x.pre(ly, first(ly, b))
                    chunks(e, ly, b, lambda k, it, par, nx, prev, last: x.main(ly, it, par, k, nx))
                    barrier(e, b * (NSTG + 2) + (2 + 3 * ly))
                    act_back(e, ly, b * 2 + ly)
                    barrier(e, b * (NSTG + 2) + (3 + 3 * ly))
                act_attn(e, b)
                barrier(e, b * (NSTG + 2) + NSTG)
                settled(e)
                e.preload_act_table_set("natural_log_exp_and_others")
                barrier(e, b * (NSTG + 2) + (NSTG + 1))
            tail(e, ActTail(), lambda *a: None, lambda *a: None)

        @block.tensor
        def _(e):
            e.wait_ge(s_w, 16 * N_WEIGHTS)
            x = Pe(e)
            with e.Fori(0, batches) as b:
                barrier(e, b * (NSTG + 2))
                for ly in range(2):
                    pe_front(e, ly, b * 2 + ly)
                    barrier(e, b * (NSTG + 2) + (1 + 3 * ly))
                    x.pre(ly, first(ly, b))
                    chunks(e, ly, b, lambda k, it, par, nx, prev, last: x.main(ly, it, par, nx, prev))
                    barrier(e, b * (NSTG + 2) + (2 + 3 * ly))
                    pe_back(e, ly, b * 2 + ly)
                    barrier(e, b * (NSTG + 2) + (3 + 3 * ly))
                pe_attn(e, b)
                barrier(e, b * (NSTG + 2) + NSTG)
                barrier(e, b * (NSTG + 2) + (NSTG + 1))
            tail(e, PeTail(), lambda *a: None, lambda *a: None)


N_WEIGHTS = 2 * 14 + 5


def kernel(**inputs):
    import numpy as np
    import concourse.bacc as _bacc
    from concourse import mybir as _mybir
    from concourse.bass_utils import run_bass_kernel_spmd as _run

    i = {k: np.asarray(v) for k, v in inputs.items()}
    B = i["x"].shape[0]

    def halves(a):
        return a.reshape(a.shape[0], 2, P, -1).transpose(2, 0, 1, 3)

    a = {"xT": i["x"].reshape(B, L, P).transpose(0, 2, 1)}
    c0, c1 = "L0_conv_", "L1_conv_"
    a["win0"], a["win1"] = i[c0 + "w_in"], i[c1 + "W_in"].T
    a["cw0"] = halves(i[c0 + "conv_w"].reshape(1, 9, DI).transpose(0, 2, 1))[:, 0]
    a["cw1"] = halves(i[c1 + "conv_w"].reshape(1, DI, 9))[:, 0]
    a["wx0"] = halves(i[c0 + "w_xproj"][None])
    a["wx1"] = halves(i[c1 + "x_proj_w"].transpose(0, 2, 1))
    a["wdt0"] = i[c0 + "w_dt"][:, None, :]
    a["wdt1"] = i[c1 + "dt_proj_w"].transpose(2, 0, 1)
    a["al0"], a["al1"] = halves(i[c0 + "A_log"][None]), halves(i[c1 + "A_logs"].reshape(K, DI, NS))
    a["dtb0"], a["dtb1"] = halves(i[c0 + "b_dt"][None])[..., 0], halves(i[c1 + "dt_proj_b"])[..., 0]
    a["dd0"], a["dd1"] = halves(i[c0 + "D_param"][None])[..., 0], halves(i[c1 + "Ds"].reshape(K, DI))[..., 0]
    for n, c in ((0, c0), (1, c1)):
        a[f"cb{n}"] = halves(i[c + "conv_b"][None])[:, 0, :, 0]
        a[f"lw{n}"] = halves(i[c + "ln_w"][None])[:, 0, :, 0]
        a[f"lb{n}"] = halves(i[c + "ln_b"][None])[:, 0, :, 0]
    a["wo0"] = halves(i[c0 + "w_out"][None])[:, 0]
    a["wo1"] = halves(i[c1 + "W_out"].T[None])[:, 0]

    def rep(v):
        return np.broadcast_to(v[..., None, :], v.shape[:-1] + (I8, A16)).reshape(v.shape[:-1] + (P,))

    w1 = i["L2_attn_W1"]
    a["w1f"], a["w1g"] = rep(w1[:P]), rep(w1[P:])
    a["b1c"], a["w2c"] = rep(i["L2_attn_b1"])[:, None], rep(i["L2_attn_w2"][:, 0])[:, None]
    a["b2c"] = np.broadcast_to(i["L2_attn_b2"][None], (P, 1))
    a["wq"], a["wk"], a["wv"] = i["L3_attn_Wq"], i["L3_attn_Wk"], i["L3_attn_Wv"]
    a["qkvb"] = np.stack([i["L3_attn_bq"], i["L3_attn_bk"], i["L3_attn_bv"]], axis=1)
    for m in (2, 3):
        c = f"L{m}_ffn_"
        u1, u2 = i[c + "weight1"], i[c + "weight2"]
        a[f"gw_{m}"] = i[c + "gate_w"].T
        a[f"gb_{m}"] = np.concatenate([i[c + "gate_b"]] * 2)[:, None]
        a[f"b1_{m}"] = u1[:, P].reshape(E64, P, 4).transpose(1, 2, 0)
        a[f"b2_{m}"] = np.concatenate([u2[:, HID]] * 2)
        a[f"u1_{m}"], a[f"u2_{m}"] = u1, u2

    nc = _bacc.Bacc("TRN2", target_bir_lowering=False, num_devices=1)
    arrays, t = {}, {}
    for name, v in a.items():
        v = np.ascontiguousarray(v)
        arrays[f"in_{name}_dram"] = v
        t[name] = nc.dram_tensor(f"in_{name}_dram", v.shape, _mybir.dt.from_np(v.dtype), kind="ExternalInput").ap()
    out = nc.dram_tensor("out_0_dram", (B, P, L), _mybir.dt.float32, kind="ExternalOutput").ap()
    res = nc.dram_tensor("residual_dram", (B, P, L), _mybir.dt.float32, kind="Internal").ap()
    program(nc, t, res, out, B)
    r = _run(nc, [arrays], core_ids=[0])
    return r.results[0]["out_0_dram"].reshape(B, P, W, W).transpose(0, 2, 3, 1)
```

```python
import math
from contextlib import ExitStack

import concourse.bass as bass
from concourse import mybir

ALU = mybir.AluOpType
ACT = mybir.ActivationFunctionType
F32 = mybir.dt.float32
BF16 = mybir.dt.bfloat16

P = 128
L = 4096
W = 64
DI = 256
NS = 16
R = 8
T = 512
NCH = L // T
TILES = 2 * NS
K = 4
NH, NG, NC, ND = 8, 4, 4, 4
PW = W + 2
CR = 64
ROWS = T // W
NSPLIT = 96

A16, I8 = 16, 8
PASS = 2048
NT = 8
E64, HID, TOP = 64, 512, 8
EG = 4
LOWEST = -3.4028234663852886e38

Y0, A0, B0, CB, MB = 0, 2, 4, 6, 7


def program(nc, t, res, out, batches):
    ctx = ExitStack()

    def sb(name, shape, dt=F32):
        return ctx.enter_context(nc.sbuf_tensor(name, shape, dt))

    with ctx:
        ps = ctx.enter_context(nc.psum_tensor("ps", [P, 8, T], F32))
        counting = []

        def sem(name, credit=True):
            s = ctx.enter_context(nc.semaphore(name))
            if credit:
                counting.append(s)
            return s

        ds = bass.ds

        ident = sb("ident", [P, P])
        group_mean = sb("group_mean", [P, P])
        mean256 = sb("mean256", [P, P])
        mean128 = sb("mean128", [P, P])
        pick = sb("pick", [NSPLIT, 32], BF16)
        keep_mid = sb("keep_mid", [NSPLIT, 1])
        keep_low = sb("keep_low", [NSPLIT, 1])
        take_high = sb("take_high", [NSPLIT, NSPLIT], BF16)
        take_mid = sb("take_mid", [NSPLIT, NSPLIT], BF16)
        eps = sb("eps", [P, 2])
        lay = []
        for n, kk in ((0, 1), (1, K)):
            lay.append(dict(
                kk=kk,
                win=sb(f"win{n}", [P, 2 * DI]), cw=sb(f"cw{n}", [P, 2, 9]), cb=sb(f"cb{n}", [P, 2]),
                wx=sb(f"wx{n}", [P, kk, 2, NSPLIT + R]), wdt=sb(f"wdt{n}", [NSPLIT + R, kk, DI]),
                dtb=sb(f"dtb{n}", [P, kk, 2]), al=sb(f"al{n}", [P, kk, 2, NS]), na=sb(f"na{n}", [P, kk, 2, NS]),
                dd=sb(f"dd{n}", [P, kk, 2]), dsum=sb(f"dsum{n}", [P, 2, 2]),
                lw=sb(f"lw{n}", [P, 2]), lb=sb(f"lb{n}", [P, 2]), wo=sb(f"wo{n}", [P, 2, P])))

        xT = sb("xT", [P, L])
        V = sb("V", [P, 2, 2, L])
        ypad = sb("ypad", [P, 2, PW * PW])
        Y = ypad[:, :, 0:L]

        delta = sb("delta", [P, 2, 2, T])
        du = sb("du", [P, 2, 2, T])
        split = sb("split", [NSPLIT, 2, T], BF16)
        tmp = sb("tmp", [P, 2, 2, T])
        high = sb("high", [NSPLIT, T], BF16)
        mid = sb("mid", [NSPLIT, T], BF16)
        ranks = sb("ranks", [NSPLIT + R, T])
        H = sb("H", [P, NH, T])
        G = sb("G", [P, NG, T])
        Cs = sb("Cs", [P, NC, T])
        dbu = sb("dbu", [P, ND, T])
        carry = sb("carry", [P, TILES])

        f_bias = dbu.rearrange("p a t -> p (a t)")[:, 0:L // I8]
        row_bias = sb("row_bias", [P, A16])
        stats = sb("stats", [P, NCH, 6])
        gn = sb("gn", [P, 8])
        xn = G[:, 0:2, :]
        diag = dbu[:, :, :].rearrange("p a t -> p (a t)")[:, 0:9 * P].rearrange("p (a t) -> p a t", a=9)
        acc = H[:, 0:4, :].rearrange("p a t -> p (a t)").rearrange("p (b t) -> p b t", b=2)

        w1f, w1g = sb("w1f", [P, P]), sb("w1g", [P, P])
        b1c, w2c, b2c = sb("b1c", [P, 1]), sb("w2c", [P, 1]), sb("b2c", [P, 1])
        own = sb("own", [P, I8])
        w2pick = sb("w2pick", [P, 4, 32])
        before = sb("before", [P, T + 3 * P], BF16)
        rden = sb("rden", [P, 2])
        a_xn, a_g = V[:, 0, 0, :], V[:, 0, 1, :]
        tok = ypad[:, 0, 0:32 * (P + 1)].rearrange("p (j d) -> p j d", j=32)
        flat = [x[:].rearrange("p a b t -> p (a b t)") for x in (tmp, delta)]
        Hf = H[:].rearrange("p a t -> p (a t)")
        tanh = [V[:, 1, i // 2, (i % 2) * PASS:(i % 2) * PASS + PASS] for i in range(4)]
        tanh += [Hf[:, 0:PASS], Hf[:, PASS:2 * PASS]] + flat
        scores = du[:].rearrange("p a b t -> p (a b t)")
        scoresT = G[:].rearrange("p a t -> p (a t)")
        att = Cs[:, 0, 0:P]
        sel = Cs[:, 1:3, :]

        Gf = G[:].rearrange("p a t -> p (a t)")
        used = [0]

        def in_g(*shape):
            n = math.prod(shape)
            v = Gf[:, used[0]:used[0] + n]
            used[0] += n
            return v if len(shape) == 1 else v.rearrange("p (a b) -> p a b", a=shape[0])

        moe = [dict(gw=in_g(E64), gb=in_g(1), b1=in_g(4, E64), b2=in_g(P)) for _ in range(2)]
        wq, wk, wv, qkvb = in_g(P), in_g(P), in_g(P), in_g(3)
        kvs = in_g(NCH + 2)
        top8 = in_g(2, TOP)
        esum = in_g(2, 3)

        s_w = sem("weights_loaded", False)
        s_const = sem("constants_made", False)
        s_aexp = sem("decay_rates_made", False)
        bar = sem("stage_ended", False)
        waits_taken = sem("waits_taken", False)
        s_x = sem("image_loaded", False)
        s_store = sem("result_stored", False)

        b_ready, dbu_done = sem("b_ready"), sem("dbu_done")
        a_ready, scan_done = sem("decay_ready"), sem("scan_done")
        c_psum, c_ready = sem("c_in_psum"), sem("c_ready")
        g_done, ysum_done = sem("g_done"), sem("ysum_done")
        evac = sem("y_added")
        carried = sem("carry_saved")
        xp_done, hi_done, rk_done, rest_done = sem("xproj_done"), sem("high_done"), sem("ranks_done"), sem("rest_done")
        mid_done, low_done, split_done = sem("mid_done"), sem("low_done"), sem("split_done")
        dt0_done, dt1_done = sem("dt0_done"), sem("dt1_done")
        ar0_done, ar1_done = sem("abs_relu0_done"), sem("abs_relu1_done")
        ex_done, lnsq_done, w_done = sem("exp_done"), sem("log_square_done"), sem("small_done")
        mx_done, delta_done, du_done = sem("max_done"), sem("delta_done"), sem("du_done")

        gn_s, gn_p, gn_v, gn_a = sem("gn_dve"), sem("gn_pe"), sem("gn_scale"), sem("gn_act")
        xn_done, pr_done, pad_done = sem("xn_done"), sem("proj_done"), sem("pad_done")
        border = sem("border_done")
        diag_done, cv_done, cvd_done, silu_done = sem("diag_done"), sem("conv_pe"), sem("conv_dve"), sem("silu_done")
        v_done, yi_done = sem("orders_done"), sem("y_started")
        zx, zp, zs = sem("z_norm"), sem("z_proj"), sem("z_silu")
        k_mu, k_yc, k_sq, k_var, k_rs = sem("mu_done"), sem("centred"), sem("squared"), sem("var_done"), sem("rstd")
        k_yn, k_yl, k_yg, k_op, k_res = sem("normed"), sem("affine"), sem("gated"), sem("out_proj"), sem("residual")

        l_mu, l_c, l_sq, l_var, l_rs, l_n = (sem("ln_mean"), sem("ln_centred"), sem("ln_squared"), sem("ln_var"),
                                             sem("ln_rstd"), sem("ln_done"))
        f_ps, f_mul, f_red = sem("f_in_psum"), sem("f_masked"), sem("f_ready")
        g_ps, g_rdy = sem("g_in_psum"), sem("g_copied")
        tk_ps, tk_rdy = sem("tokens_in_psum"), sem("tokens_ready")
        rb_done, th_done, sc_mm = sem("row_bias_ready"), sem("tanh_done"), sem("tanh_group_read")
        e_done, m_done = sem("scores_exp"), sem("scores_masked")
        t_ps, t_sb, o_mm, o_ps = sem("scores_turned"), sem("turned_copied"), sem("turned_read"), sem("attended")
        den_s, att_s, at_ps, at_add = sem("denominator"), sem("attended_scaled"), sem("attended_turned"), sem("attended_added")

        lg_ps, lg_rdy = sem("logits_in_psum"), sem("logits_ready")
        r_max, r_mark, r_neg, r_exp, r_inv, r_w, r_scaled = (sem("top8_found"), sem("top8_marked"), sem("minus_max"),
                                                             sem("logits_exp"), sem("inverse_sum"), sem("routed"), sem("weights_scaled"))
        c_tok_ps, c_w_ps, c_tok, c_w, c_mm, c_out = (sem("block_tokens_psum"), sem("block_weights_psum"), sem("block_tokens"),
                                                     sem("block_weights"), sem("block_pooled"), sem("pooled_copied"))
        d_w1 = [sem(f"w1_loaded{u}", False) for u in range(2)]
        d_w2 = [sem(f"w2_loaded{u}", False) for u in range(2)]
        d_h, d_hb, d_hT, d_o = sem("hidden_in_psum"), sem("hidden_biased"), sem("hidden_ready"), sem("experts_used")
        d_in, d_raw, d_th, d_oc, d_to, d_ot = (sem("group_ready"), sem("hidden_copied"), sem("hidden_turned"), sem("output_copied"),
                                         sem("output_turned"), sem("output_kept"))
        o_t, o_b = sem("out_turned"), sem("out_biased")
        f_ps2, f_add = sem("scattered"), sem("scatter_added")
        q_ps, q_v, q_kv, q_sum, q_out, q_add = (sem("kv_in_psum"), sem("v_ready"), sem("kv_summed"), sem("kv_total"),
                                                sem("q_scaled"), sem("q_added"))
        qq_ps = sem("q_in_psum")

        block = ctx.enter_context(nc.Block())

        def settled(e):
            e.sem_inc(waits_taken, 1)

        def barrier(e, n):
            settled(e)
            e.drain().then_inc(bar, 1)
            e.wait_ge(bar, n * 5 + 5)
            settled(e)

        def at(it, n=0, per=1):
            return it * per + (CR + n + 1)

        def order(k, c):
            if k < 2:
                return V[:, k, :, ds(c * T, T)]
            return V[:, k - 2, :, ds((NCH - 1) * T - c * T, T)]

        def turned(k, v):
            return v if k < 2 else (v[:, :, ::-1] if len(v.shape) == 3 else v[:, ::-1])

        def image(k, c):
            if k % 2 == 0:
                a = c * T if k == 0 else (NCH - 1) * T - c * T
                return Y[:, :, ds(a, T)].rearrange("p s (a b) -> p s a b", a=ROWS)
            a = c * ROWS if k == 1 else W - ROWS - c * ROWS
            return Y.rearrange("p s (h w) -> p s w h", w=W)[:, :, ds(a, ROWS), :]

        def kof(ly, k):
            return k if lay[ly]["kk"] == K else 0

        class Pe:
            def __init__(s, e):
                s.e = e

            def xproj(s, ly, nx):
                k, c, it = nx
                e, w = s.e, lay[ly]
                e.wait_ge(ar1_done, at(it) - 1)
                src = order(0, c) if ly == 0 else order(k, c)
                for h in range(2):
                    m = e.matmul(ps[0:NSPLIT + R, MB, :], w["wx"][:, kof(ly, k), h, :], src[:, h, :],
                                 start=(h == 0), stop=(h == 1))
                m.then_inc(xp_done, 1)

            def less_high(s, nx):
                e, it = s.e, nx[2]
                e.wait_ge(rk_done, at(it))
                e.wait_ge(hi_done, at(it))
                e.matmul(ps[0:NSPLIT, MB, :], take_high[:, :], high[:, :], start=False, stop=True,
                         skip_group_check=True).then_inc(rest_done, 1)

            def less_mid(s, nx):
                e, it = s.e, nx[2]
                e.wait_ge(mid_done, at(it))
                e.matmul(ps[0:NSPLIT, MB, :], take_mid[:, :], mid[:, :], start=False, stop=True,
                         skip_group_check=True).then_inc(low_done, 1)

            def dt(s, ly, nx, h):
                k, c, it = nx
                e, w = s.e, lay[ly]
                if h == 0:
                    e.wait_ge(split_done, at(it))
                else:
                    e.wait_ge(ar0_done, at(it))
                e.matmul(ps[:, MB, :], w["wdt"][NSPLIT:, kof(ly, k), h * P:h * P + P], ranks[NSPLIT:, :],
                         start=True, stop=True).then_inc(dt1_done if h else dt0_done, 1)

            def bc(s, it, n, par):
                e = s.e
                if n == 0:
                    e.wait_ge(split_done, at(it))
                e.wait_ge(dbu_done, at(it, 2 * n + 1 - 4, TILES))
                e.matmul(ps[:, B0 + n % 2, :], pick[:, n:n + 1].to_broadcast([NSPLIT, P]), split[:, par, :], start=True, stop=True).then_inc(b_ready, 1)
                e.wait_ge(c_ready, at(it, n - 1, NS))
                e.matmul(ps[:, CB, :], pick[:, NS + n:NS + n + 1].to_broadcast([NSPLIT, P]), split[:, par, :], start=True, stop=True).then_inc(c_psum, 1)

            def ysum(s, k, c, it, n):
                e = s.e
                if n == 0:
                    e.wait_ge(evac, at(it) - 1)
                if n == NS // 2:
                    for h in range(2):
                        e.matmul(turned(k, ps[:, Y0 + h, :]).rearrange("p (a b) -> p a b", a=ROWS), ident[:, :],
                                 image(k, c)[:, h], start=False, stop=False)
                for h in range(2):
                    j = 2 * n + h
                    e.wait_ge(g_done, at(it, j, TILES))
                    e.matmul(ps[:, Y0 + h, :], ident[:, :], G[:, j % NG, :],
                             start=(n == 0), stop=(n == NS - 1)).then_inc(ysum_done, 1)

            def pre(s, ly, nx):
                s.xproj(ly, nx)
                s.less_high(nx)
                s.less_mid(nx)
                s.dt(ly, nx, 0)
                s.dt(ly, nx, 1)
                s.bc(nx[2], 0, 0)
                s.bc(nx[2], 1, 0)

            def main(s, ly, k, c, it, par, nx):
                for n in range(NS):
                    if n < NS - 2:
                        s.bc(it, n + 2, par)
                    elif nx:
                        s.bc(nx[2], n + 2 - NS, 1 - par)
                    if nx and n == 0:
                        s.xproj(ly, nx)
                    if nx and n == 2:
                        s.less_high(nx)
                    if nx and n == 3:
                        s.less_mid(nx)
                    if nx and n in (5, 7):
                        s.dt(ly, nx, (n - 5) // 2)
                    s.ysum(k, c, it, n)

        class Act:
            def __init__(s, e):
                s.e = e

            def split_high(s, ly, nx):
                e, it = s.e, nx[2]
                e.wait_ge(xp_done, at(it))
                e.activation(high[:, :], ps[0:NSPLIT, MB, :], ACT.Copy).then_inc(hi_done, 1)
                e.activation(ranks[NSPLIT:, :], turned(nx[0] * ly, ps[NSPLIT:NSPLIT + R, MB, :]), ACT.Copy).then_inc(rk_done, 1)

            def split_mid(s, nx):
                e, it = s.e, nx[2]
                e.wait_ge(rest_done, at(it))
                e.activation(mid[:, :], ps[0:NSPLIT, MB, :], ACT.Copy).then_inc(mid_done, 1)

            def split_low(s, ly, nx, par):
                e, it = s.e, nx[2]
                e.wait_ge(low_done, at(it))
                e.activation(split[:, par, :], turned(nx[0] * ly, ps[0:NSPLIT, MB, :]), ACT.Copy).then_inc(split_done, 1)

            def abs_relu(s, ly, nx, h, par):
                e, (k, c, it) = s.e, nx
                bias = lay[ly]["dtb"][:, kof(ly, k), h:h + 1]
                e.wait_ge(dt1_done if h else dt0_done, at(it))
                if h == 0:
                    e.wait_ge(delta_done, at(it) - 1)
                e.activation(tmp[:, 0, h, :], ps[:, MB, :], ACT.Abs, bias=bias)
                e.activation(delta[:, par, h, :], ps[:, MB, :], ACT.Relu, bias=bias).then_inc(ar1_done if h else ar0_done, 1)

            def exp(s, nx):
                e, it = s.e, nx[2]
                e.wait_ge(ar1_done, at(it))
                e.activation(tmp[:, 0], tmp[:, 0], ACT.Exp, scale=-1.0).then_inc(ex_done, 1)

            def log(s, nx):
                e, it = s.e, nx[2]
                e.wait_ge(ex_done, at(it))
                e.activation(tmp[:, 1], tmp[:, 0], ACT.Ln, bias=1.0)

            def square(s, nx, par):
                s.e.activation(du[:, par], tmp[:, 0], ACT.Square, scale=math.sqrt(0.5)).then_inc(lnsq_done, 1)

            def pre(s, ly, nx):
                s.split_high(ly, nx)
                s.split_mid(nx)
                s.split_low(ly, nx, 0)
                s.abs_relu(ly, nx, 0, 0)
                s.abs_relu(ly, nx, 1, 0)
                s.exp(nx)
                s.log(nx)
                s.square(nx, 0)

            def keep_y(s, prev):
                e, (k, c, it) = s.e, prev
                e.wait_ge(ysum_done, at(it, TILES - 1, TILES))
                e.activation(image(k, c), turned(k, ps[:, Y0:Y0 + 2, :]).rearrange("p s (a b) -> p s a b", a=ROWS),
                             ACT.Copy).then_inc(evac, 1)

            def main(s, ly, it, par, k, nx, prev):
                e, w = s.e, lay[ly]
                for n in range(NS):
                    e.wait_ge(c_psum, at(it, n, NS))
                    e.wait_ge(g_done, at(it, 2 * (n - NC) + 1, TILES))
                    e.activation(Cs[:, n % NC, :], ps[:, CB, :], ACT.Copy).then_inc(c_ready, 1)
                    if n == 0:
                        e.wait_ge(delta_done, at(it))
                    for h in range(2):
                        j = 2 * n + h
                        e.wait_ge(scan_done, at(it, j - 2, TILES))
                        e.activation(ps[:, A0 + j % 2, :], delta[:, par, h, :], ACT.Exp,
                                     scale=w["na"][:, kof(ly, k), h, n:n + 1]).then_inc(a_ready, 1)
                        if j == 3 and prev:
                            s.keep_y(prev)
                    if nx:
                        if n == 1:
                            s.split_high(ly, nx)
                        if n == 3:
                            s.split_mid(nx)
                        if n == 4:
                            s.split_low(ly, nx, 1 - par)
                        if n in (6, 8):
                            s.abs_relu(ly, nx, (n - 6) // 2, 1 - par)
                        if n == 9:
                            s.exp(nx)
                        if n == 10:
                            s.log(nx)
                        if n == 11:
                            s.square(nx, 1 - par)

        class Dve:
            def __init__(s, e):
                s.e = e

            def softplus_max(s, nx, par):
                e, it = s.e, nx[2]
                e.wait_ge(w_done, at(it))
                e.tensor_tensor(tmp[:, 1], tmp[:, 1], du[:, par], ALU.max).then_inc(mx_done, 1)

            def softplus_add(s, nx, par):
                e, it = s.e, nx[2]
                e.wait_ge(mx_done, at(it))
                e.tensor_tensor(delta[:, par], tmp[:, 1], delta[:, par], ALU.add).then_inc(delta_done, 1)

            def mult(s, it, j, par):
                e = s.e
                n, h = j // 2, j % 2
                if j < 2:
                    e.wait_ge(du_done, at(it, j, 2))
                if h == 0:
                    e.wait_ge(b_ready, at(it, n, NS))
                e.wait_ge(scan_done, at(it, j - ND, TILES))
                e.tensor_tensor(dbu[:, j % ND, :], du[:, par, h, :], ps[:, B0 + n % 2, :], ALU.mult).then_inc(dbu_done, 1)

            def scan(s, it, j):
                e = s.e
                e.wait_ge(a_ready, at(it, j, TILES))
                e.wait_ge(dbu_done, at(it, j, TILES))
                e.wait_ge(g_done, at(it, j - NH, TILES))
                e.tensor_tensor_scan(H[:, j % NH, :], ps[:, A0 + j % 2, :], dbu[:, j % ND, :], carry[:, j:j + 1],
                                     ALU.mult, ALU.add).then_inc(scan_done, 1)

            def store_states(s, it, g):
                e = s.e
                e.wait_ge(scan_done, at(it, 4 * g + 3, TILES))
                a = (4 * g) % NH
                e.tensor_copy(carry[:, 4 * g:4 * g + 4], H[:, a:a + 4, T - 1]).then_inc(carried, 1)

            def pre(s, ly, nx):
                s.softplus_max(nx, 0)
                s.softplus_add(nx, 0)
                s.e.memset(carry[:, :], 0.0).then_inc(carried, TILES // 4)
                s.mult(nx[2], 0, 0)

            def main(s, ly, it, par, nx, last):
                e = s.e
                for j in range(TILES):
                    if j + 1 < TILES:
                        s.mult(it, j + 1, par)
                    elif nx:
                        s.mult(nx[2], 0, 1 - par)
                    if j == 0:
                        e.wait_ge(carried, at(it, TILES // 4 - 1, TILES // 4))
                    s.scan(it, j)
                    if j % 4 == 0 and j and not last:
                        s.store_states(it, j // 4 - 1)
                    if nx:
                        if j == 26:
                            s.softplus_max(nx, 1 - par)
                        if j == 27:
                            s.softplus_add(nx, 1 - par)
                if not last:
                    s.store_states(it, TILES // 4 - 1)
                elif nx:
                    e.wait_ge(scan_done, at(it, TILES - 1, TILES))
                    e.memset(carry[:, :], 0.0).then_inc(carried, TILES // 4)

        class Pool:
            def __init__(s, e):
                s.e = e

            def small(s, nx, par):
                e, it = s.e, nx[2]
                e.wait_ge(lnsq_done, at(it))
                e.tensor_tensor(du[:, par], tmp[:, 0], du[:, par], ALU.subtract).then_inc(w_done, 1)

            def inputs(s, nx, par, h):
                e, (k, c, it) = s.e, nx
                e.wait_ge(delta_done, at(it))
                e.tensor_tensor(turned(k, du[:, par, h]), turned(k, delta[:, par, h]), order(k, c)[:, h], ALU.mult).then_inc(du_done, 1)

            def pre(s, ly, nx):
                s.small(nx, 0)
                s.inputs(nx, 0, 0)
                s.inputs(nx, 0, 1)

            def main(s, it, par, nx):
                e = s.e
                for j in range(TILES):
                    n = j // 2
                    if j % 2 == 0:
                        e.wait_ge(c_ready, at(it, n, NS))
                    e.wait_ge(scan_done, at(it, j, TILES))
                    e.wait_ge(ysum_done, at(it, j - NG, TILES))
                    e.tensor_tensor(G[:, j % NG, :], H[:, j % NH, :], Cs[:, n % NC, :], ALU.mult).then_inc(g_done, 1)
                    if nx:
                        if j == 22:
                            s.small(nx, 1 - par)
                        if j in (28, 29):
                            s.inputs(nx, 1 - par, j - 28)

        def chunks(e, ly, b, run):
            base = b * (2 * K * NCH) + ly * K * NCH
            for k in range(K):
                it = base + k * NCH
                run(k, 0, it, 0, (k, 1, it + 1), (k - 1, NCH - 1, it - 1) if k else None, False)
                settled(e)
                with e.Fori(0, (NCH - 2) // 2) as p:
                    for u in range(2):
                        c = 2 * p + (1 + u)
                        i = it + c
                        run(k, c, i, 1 - u, (k, c + 1, i + 1), (k, c - 1, i - 1), False)
                i = it + (NCH - 1)
                run(k, NCH - 1, i, 1, (k + 1, 0, i + 1) if k + 1 < K else None, (k, NCH - 2, i - 1), True)
            return base

        def first(ly, b):
            return (0, 0, b * (2 * K * NCH) + ly * K * NCH)

        def of(q, n, per):
            return q * per + (CR + n + 1)

        padv = ypad[:, :, :].rearrange("p s (a b) -> p s a b", a=PW)
        CP = 4
        turns = [(0, 0), (1, 0), (0, 1), (1, 1), (0, 2), (0, 3), (1, 2), (0, 4), (1, 3), (0, 5), (0, 6), (0, 7)]
        assert len(turns) == NCH + CP

        def silu_of(q, h, c):
            return of(q, turns.index((h, c)), NCH + CP)


        def dve_front(e, ly, q):
            w = lay[ly]
            for c in range(NCH):
                i = e.bn_stats(stats[:, c, :], xT[:, c * T:c * T + T])
            i.then_inc(gn_s, 1)
            e.wait_ge(gn_s, of(q, 0, 3))
            settled(e)
            e.bn_aggr(gn[:, 0:2], stats[:, :, :].rearrange("p a b -> p (a b)")).then_inc(gn_s, 1)
            e.memset(padv[:, :, 0:PW:PW - 1, :], 0.0)
            e.memset(padv[:, :, 1:PW - 1, 0:PW:PW - 1], 0.0).then_inc(border, 1)
            e.wait_ge(gn_p, of(q, 0, 2))
            e.tensor_copy(gn[:, 2:4], ps[:, 0, 0:2]).then_inc(gn_v, 1)
            e.wait_ge(gn_v, of(q, 0, 4))
            e.tensor_tensor(gn[:, 4:5], gn[:, 0:1], gn[:, 2:3], ALU.subtract).then_inc(gn_v, 1)
            e.wait_ge(gn_v, of(q, 1, 4))
            e.tensor_tensor(gn[:, 5:6], gn[:, 4:5], gn[:, 4:5], ALU.mult).then_inc(gn_s, 1)
            e.wait_ge(gn_p, of(q, 1, 2))
            e.tensor_tensor(gn[:, 4:5], gn[:, 3:4], ps[:, 0, 2:3], ALU.add).then_inc(gn_v, 1)
            e.wait_ge(gn_a, of(q, 1, 2))
            e.scalar_tensor_tensor(gn[:, 7:8], gn[:, 2:3], -1.0, gn[:, 6:7], ALU.mult, ALU.mult).then_inc(gn_v, 1)
            for tap in range(9):
                i = e.tensor_scalar(diag[:, tap, :], ident[:, :], w["cw"][:, 0, tap:tap + 1], None, ALU.mult)
            i.then_inc(diag_done, 1)
            e.wait_ge(gn_v, of(q, 3, 4))
            for c in range(NCH):
                if c >= 2:
                    e.wait_ge(pr_done, of(q, 2 * (c - 2) + 1, 2 * NCH))
                e.tensor_scalar(xn[:, c % 2, :], xT[:, c * T:c * T + T], gn[:, 6:7], gn[:, 7:8],
                                ALU.mult, ALU.add).then_inc(xn_done, 1)
            for p in range(CP):
                last = min(2 * p + 2, NCH - 1)
                e.wait_ge(pad_done, of(q, 2 * last + 1, 2 * NCH))
                if p >= 2:
                    e.wait_ge(silu_done, silu_of(q, 1, p - 2))
                dst = acc[:, p % 2, :].rearrange("p (a b) -> p a b", a=16)
                for tap in range(9):
                    src = padv[:, 1, 16 * p + tap // 3:16 * p + tap // 3 + 16, tap % 3:tap % 3 + W]
                    if tap == 0:
                        e.tensor_scalar(dst, src, w["cw"][:, 1, 0:1], w["cb"][:, 1:2], ALU.mult, ALU.add).then_inc(cvd_done, 1)
                    else:
                        e.wait_ge(cvd_done, of(q, 9 * p + tap - 1, 9 * CP))
                        e.scalar_tensor_tensor(dst, src, w["cw"][:, 1, tap:tap + 1], dst, ALU.mult, ALU.add).then_inc(cvd_done, 1)
            for n, h in enumerate((1, 0)):
                e.wait_ge(v_done, of(q, 4 * n + 3, 8))
                if h == 0:
                    e.wait_ge(cv_done, of(q, NCH - 1, NCH))
                else:
                    e.wait_ge(cvd_done, of(q, 9 * CP - 1, 9 * CP))
                e.tensor_scalar(Y[:, h, :], V[:, 0, h, :], w["dsum"][:, 0, h:h + 1], None, ALU.mult).then_inc(yi_done, 1)
                e.wait_ge(yi_done, of(q, 2 * n, 4))
                yv = Y[:, h, :].rearrange("p (h w) -> p w h", w=W)
                e.scalar_tensor_tensor(yv, V[:, 1, h, :].rearrange("p (w h) -> p w h", w=W), w["dsum"][:, 1, h:h + 1],
                                       yv, ALU.mult, ALU.add).then_inc(yi_done, 1)

        def pe_front(e, ly, q):
            w = lay[ly]
            e.wait_ge(gn_s, of(q, 1, 3))
            e.matmul(ps[:, 0, 0:2], group_mean[:, :], gn[:, 0:2], start=True, stop=True).then_inc(gn_p, 1)
            e.wait_ge(gn_s, of(q, 2, 3))
            e.matmul(ps[:, 0, 2:3], group_mean[:, :], gn[:, 5:6], start=True, stop=True).then_inc(gn_p, 1)
            for c in range(NCH):
                e.wait_ge(xn_done, of(q, c, NCH))
                for h in range(2):
                    if c >= 2:
                        e.wait_ge(pad_done, of(q, 2 * (c - 2) + h, 2 * NCH))
                    e.matmul(ps[:, 2 + 2 * (c % 2) + h, :], w["win"][:, h * P:h * P + P], xn[:, c % 2, :],
                             start=True, stop=True).then_inc(pr_done, 1)
            e.wait_ge(diag_done, of(q, 0, 1))
            for c in range(NCH):
                e.wait_ge(pad_done, of(q, 2 * min(c + 1, NCH - 1), 2 * NCH))
                if c >= 2:
                    e.wait_ge(silu_done, silu_of(q, 0, c - 2))
                for tap in range(9):
                    a = ROWS * c + tap // 3
                    m = e.matmul(ps[:, 6 + c % 2, :], diag[:, tap, :], padv[:, 0, a:a + ROWS, tap % 3:tap % 3 + W],
                                 start=(tap == 0), stop=(tap == 8))
                m.then_inc(cv_done, 1)

        def act_front(e, ly, q):
            w = lay[ly]
            e.wait_ge(gn_v, of(q, 2, 4))
            e.activation(gn[:, 6:7], gn[:, 4:5], ACT.Ln, bias=eps[:, 0:1]).then_inc(gn_a, 1)
            e.wait_ge(gn_a, of(q, 0, 2))
            e.activation(gn[:, 6:7], gn[:, 6:7], ACT.Exp, scale=-0.5).then_inc(gn_a, 1)
            e.wait_ge(border, of(q, 0, 1))
            for c in range(NCH):
                for h in range(2):
                    e.wait_ge(pr_done, of(q, 2 * c + h, 2 * NCH))
                    e.activation(padv[:, h, 1 + ROWS * c:1 + ROWS * c + ROWS, 1:1 + W],
                                 ps[:, 2 + 2 * (c % 2) + h, :].rearrange("p (a b) -> p a b", a=ROWS),
                                 ACT.Copy).then_inc(pad_done, 1)

            def silu(dst_h, row, rows, src, bias):
                if ly == 0:
                    e.activation(V[:, 0, dst_h, row * W:(row + rows) * W], src, ACT.Silu, bias=bias).then_inc(silu_done, 1)
                else:
                    hg, wh = row // 16, row % 16
                    v = V[:, 0, dst_h, hg * 1024:hg * 1024 + 1024].rearrange("p (g a b) -> p a g b", g=4, a=16)
                    e.activation(v[:, wh:wh + rows], src.rearrange("p (a g b) -> p a g b", a=rows, g=4),
                                 ACT.Silu, bias=bias).then_inc(silu_done, 1)

            def second_order(h):
                e.wait_ge(silu_done, silu_of(q, h, (NCH, CP)[h] - 1))
                for g in range(4):
                    dst = V[:, 1, h, g * 1024:g * 1024 + 1024]
                    if ly == 0:
                        src = V[:, 0, h, :].rearrange("p (h w) -> p w h", w=W)[:, 16 * g:16 * g + 16, :]
                        dst = dst.rearrange("p (w h) -> p w h", w=16)
                    else:
                        src = V[:, 0, h, :].rearrange("p (a g h w) -> p g a w h", a=4, g=4, h=16)[:, g]
                        dst = dst.rearrange("p (a w h) -> p a w h", a=4, w=16)
                    e.activation(dst, src, ACT.Copy).then_inc(v_done, 1)

            for h, c in turns:
                if h == 0:
                    e.wait_ge(cv_done, of(q, c, NCH))
                    silu(0, ROWS * c, ROWS, ps[:, 6 + c % 2, :], w["cb"][:, 0:1])
                else:
                    e.wait_ge(cvd_done, of(q, 9 * c + 8, 9 * CP))
                    silu(1, 16 * c, 16, acc[:, c % 2, :], 0.0)
                    if c == CP - 1:
                        second_order(1)
            second_order(0)

        def dve_back(e, ly, q):
            for c in range(NCH):
                if c >= 2:
                    e.wait_ge(zp, of(q, 2 * (c - 2) + 1, 2 * NCH))
                e.tensor_scalar(xn[:, c % 2, :], xT[:, c * T:c * T + T], gn[:, 6:7], gn[:, 7:8],
                                ALU.mult, ALU.add).then_inc(zx, 1)
            yc, yn = delta, du

            def centre(c):
                e.wait_ge(k_mu, of(q, c, NCH))
                if c >= 2:
                    e.wait_ge(k_yn, of(q, 2 * (c - 2) + 1, 2 * NCH))
                for h in range(2):
                    e.tensor_tensor(yc[:, c % 2, h, :], Y[:, h, c * T:c * T + T], ps[:, c % 2, :], ALU.subtract).then_inc(k_yc, 1)

            def norm(c):
                e.wait_ge(k_rs, of(q, 2 * c + 1, 2 * NCH))
                if c >= 2:
                    e.wait_ge(k_op, of(q, c - 2, NCH))
                for h in range(2):
                    e.tensor_tensor(yn[:, c % 2, h, :], yc[:, c % 2, h, :], H[:, c % 2, :], ALU.mult).then_inc(k_yn, 1)

            def gate(c):
                for h in range(2):
                    e.wait_ge(k_yl, of(q, 2 * c + h, 2 * NCH))
                e.tensor_tensor(yn[:, c % 2], yn[:, c % 2], V[:, 0, :, c * T:c * T + T], ALU.mult).then_inc(k_yg, 1)

            def add(c):
                e.wait_ge(k_op, of(q, c, NCH))
                e.tensor_tensor(xT[:, c * T:c * T + T], xT[:, c * T:c * T + T], ps[:, 4 + c % 2, :], ALU.add).then_inc(k_res, 1)

            for i in range(NCH + 3):
                if i < NCH:
                    centre(i)
                if 1 <= i <= NCH:
                    norm(i - 1)
                if 2 <= i <= NCH + 1:
                    gate(i - 2)
                if i >= 3:
                    add(i - 3)

        def pe_back(e, ly, q):
            w = lay[ly]
            for c in range(NCH):
                e.wait_ge(zx, of(q, c, NCH))
                for h in range(2):
                    if c >= 2:
                        e.wait_ge(zs, of(q, 2 * (c - 2) + h, 2 * NCH))
                    e.matmul(ps[:, 2 + 2 * (c % 2) + h, :], w["win"][:, DI + h * P:DI + h * P + P], xn[:, c % 2, :],
                             start=True, stop=True).then_inc(zp, 1)
            for h in range(2):
                e.wait_ge(zs, of(q, 2 * NCH - 1, 2 * NCH))

            def mu(c):
                if c >= 2:
                    e.wait_ge(k_yc, of(q, 2 * (c - 2) + 1, 2 * NCH))
                for h in range(2):
                    m = e.matmul(ps[:, c % 2, :], mean256[:, :], Y[:, h, c * T:c * T + T], start=(h == 0), stop=(h == 1))
                m.then_inc(k_mu, 1)

            def var(c):
                e.wait_ge(k_sq, of(q, c, NCH))
                if c >= 2:
                    e.wait_ge(k_rs, of(q, 2 * (c - 2), 2 * NCH))
                for h in range(2):
                    m = e.matmul(ps[:, 2 + c % 2, :], mean256[:, :], tmp[:, c % 2, h, :], start=(h == 0), stop=(h == 1))
                m.then_inc(k_var, 1)

            def outp(c):
                e.wait_ge(k_yg, of(q, c, NCH))
                if c >= 2:
                    e.wait_ge(k_res, of(q, c - 2, NCH))
                for h in range(2):
                    m = e.matmul(ps[:, 4 + c % 2, :], w["wo"][:, h, :], du[:, c % 2, h, :], start=(h == 0), stop=(h == 1))
                m.then_inc(k_op, 1)

            for i in range(NCH + 3):
                if i < NCH:
                    mu(i)
                if 1 <= i <= NCH:
                    var(i - 1)
                if i >= 3:
                    outp(i - 3)

        def act_back(e, ly, q):
            w = lay[ly]
            for c in range(NCH):
                for h in range(2):
                    e.wait_ge(zp, of(q, 2 * c + h, 2 * NCH))
                    e.activation(V[:, 0, h, c * T:c * T + T], ps[:, 2 + 2 * (c % 2) + h, :], ACT.Silu).then_inc(zs, 1)
            settled(e)
            e.preload_act_table_set("natural_log_exp_and_others")

            def square(c):
                e.wait_ge(k_yc, of(q, 2 * c + 1, 2 * NCH))
                if c >= 2:
                    e.wait_ge(k_var, of(q, c - 2, NCH))
                e.activation(tmp[:, c % 2], delta[:, c % 2], ACT.Square).then_inc(k_sq, 1)

            def rstd(c):
                e.wait_ge(k_var, of(q, c, NCH))
                if c >= 2:
                    e.wait_ge(k_yn, of(q, 2 * (c - 2) + 1, 2 * NCH))
                e.activation(H[:, 2 + c % 2, :], ps[:, 2 + c % 2, :], ACT.Ln, bias=eps[:, 0:1]).then_inc(k_rs, 1)
                e.wait_ge(k_rs, of(q, 2 * c, 2 * NCH))
                e.activation(H[:, c % 2, :], H[:, 2 + c % 2, :], ACT.Exp, scale=-0.5).then_inc(k_rs, 1)

            def affine(c):
                for h in range(2):
                    e.wait_ge(k_yn, of(q, 2 * c + h, 2 * NCH))
                    e.activation(du[:, c % 2, h, :], du[:, c % 2, h, :], ACT.Identity, scale=w["lw"][:, h:h + 1],
                                 bias=w["lb"][:, h:h + 1]).then_inc(k_yl, 1)

            for i in range(NCH + 2):
                if i < NCH:
                    square(i)
                if 1 <= i <= NCH:
                    rstd(i - 1)
                if i >= 2:
                    affine(i - 2)

        def ln_pe(e, q, src):
            def mu(c):
                if c >= 2:
                    e.wait_ge(l_c, of(q, c - 2, NCH))
                e.matmul(ps[:, c % 2, :], mean128[:, :], src(c), start=True, stop=True).then_inc(l_mu, 1)

            def var(c):
                e.wait_ge(l_sq, of(q, c, NCH))
                if c >= 2:
                    e.wait_ge(l_rs, of(q, 2 * (c - 2), 2 * NCH))
                e.matmul(ps[:, 2 + c % 2, :], mean128[:, :], tmp[:, c % 2, 0, :], start=True, stop=True).then_inc(l_var, 1)

            for i in range(NCH + 1):
                if i < NCH:
                    mu(i)
                if i >= 1:
                    var(i - 1)

        def ln_act(e, q, dst):
            for i in range(NCH + 1):
                if i < NCH:
                    e.wait_ge(l_c, of(q, i, NCH))
                    if i >= 2:
                        e.wait_ge(l_var, of(q, i - 2, NCH))
                    e.activation(tmp[:, i % 2, 0, :], dst(i), ACT.Square).then_inc(l_sq, 1)
                if i >= 1:
                    c = i - 1
                    e.wait_ge(l_var, of(q, c, NCH))
                    if c >= 2:
                        e.wait_ge(l_n, of(q, c - 2, NCH))
                    e.activation(H[:, 2 + c % 2, :], ps[:, 2 + c % 2, :], ACT.Ln, bias=eps[:, 0:1]).then_inc(l_rs, 1)
                    e.wait_ge(l_rs, of(q, 2 * c, 2 * NCH))
                    e.activation(H[:, c % 2, :], H[:, 2 + c % 2, :], ACT.Exp, scale=-0.5).then_inc(l_rs, 1)

        def ln_dve(e, q, src, dst):
            for i in range(NCH + 1):
                if i < NCH:
                    e.wait_ge(l_mu, of(q, i, NCH))
                    e.tensor_tensor(dst(i), src(i), ps[:, i % 2, :], ALU.subtract).then_inc(l_c, 1)
                if i >= 1:
                    c = i - 1
                    e.wait_ge(l_rs, of(q, 2 * c + 1, 2 * NCH))
                    e.tensor_tensor(dst(c), dst(c), H[:, c % 2, :], ALU.mult).then_inc(l_n, 1)

        def cols(v):
            return lambda c: v[:, c * T:c * T + T]

        JB = L // T
        passes = [(J, off, min(PASS, J * T - off)) for J in range(1, JB + 1) for off in range(0, J * T, PASS)]
        NP1 = [len([x for x in passes if x[0] == J]) for J in range(1, JB + 1)]
        TOT_P = 4 * sum(NP1)
        TOT_B = 4 * sum(J * 4 for J in range(1, JB + 1)) // 4

        def walk(e, b, run):
            np_, nb_ = 0, 0
            for J in range(1, JB + 1):
                mine = [x for x in passes if x[0] == J]
                settled(e)
                with e.Fori(0, 4) as r:
                    p0 = b * TOT_P + (r * len(mine) + np_)
                    b0 = b * TOT_B + (r * J + nb_)
                    run(J, r, b * 32 + (r + 4 * (J - 1)), [(off, N, p0 + i, b0 + off // T) for i, (_, off, N) in enumerate(mine)])
                np_ += 4 * len(mine)
                nb_ += 4 * J

        def walk_ahead(e, b, run, finish):
            np_, nb_, prev = 0, 0, None
            for J in range(1, JB + 1):
                mine = [x for x in passes if x[0] == J]

                def one(r, prev):
                    p0 = b * TOT_P + (r * len(mine) + np_)
                    b0 = b * TOT_B + (r * J + nb_)
                    run(J, r, b * 32 + (r + 4 * (J - 1)), [(off, N, p0 + i, b0 + off // T) for i, (_, off, N) in enumerate(mine)], prev)

                def before(r):
                    _, off, N = mine[-1]
                    return (J, b * 32 + (r + 4 * (J - 1)),
                            (off, N, b * TOT_P + (r * len(mine) + (np_ + len(mine) - 1)), b * TOT_B + (r * J + (nb_ + off // T))))

                one(0, prev)
                settled(e)
                with e.Fori(0, 3) as r:
                    one(r + 1, before(r))
                prev = before(3)
                np_ += 4 * len(mine)
                nb_ += 4 * J
            finish(prev)

        def val(i, per=1, n=0):
            return i * per + (CR + n + 1)

        def pe_attn(e, b):
            ln_pe(e, b, cols(xT))
            for c in range(NCH):
                e.wait_ge(l_n, of(b, c, NCH))
                if c >= 2:
                    e.wait_ge(f_mul, of(b, c - 2, NCH))
                e.matmul(ps[:, 4 + c % 2, :], w1f[:, :], a_xn[:, c * T:c * T + T], start=True, stop=True).then_inc(f_ps, 1)
                if c >= 2:
                    e.wait_ge(g_rdy, of(b, c - 2, NCH))
                e.matmul(ps[:, 6 + c % 2, :], w1g[:, :], a_xn[:, c * T:c * T + T], start=True, stop=True).then_inc(g_ps, 1)
            e.wait_ge(l_rs, of(b, 2 * NCH - 1, 2 * NCH))
            for c in range(NCH):
                if c >= 2:
                    e.wait_ge(tk_rdy, of(b, c - 2, NCH))
                for i in range(4):
                    a = c * T + i * P
                    m = e.transpose(ps[:, c % 2, i * P:i * P + P], a_xn[:, a:a + P], ident[:, :])
                m.then_inc(tk_ps, 1)
            e.wait_ge(tk_rdy, of(b, NCH - 1, NCH))
            e.wait_ge(f_red, of(b, NCH - 1, NCH))
            e.wait_ge(g_rdy, of(b, NCH - 1, NCH))

            def block_(J, r, blk, mine, prev):
                for i, (off, N, p, bank) in enumerate(mine):
                    if i:
                        prev = (J, blk, mine[i - 1])
                    e.wait_ge(e_done, val(p) - 1)
                    for u in range(4):
                        e.wait_ge(th_done, val(p, 16, 4 * u + 3))
                        for x in range(N // T):
                            for c in range(4):
                                m = e.matmul(ps[32 * c:32 * c + 32, x, :], w2pick[:, u, :],
                                             tanh[(4 * u + c) % NT][:, x * T:x * T + T], start=(u == 0), stop=(u == 3))
                        m.then_inc(sc_mm, 1)
                        if prev and u == 1:
                            attend(*prev)
                        if prev and u == 2 and i == 0:
                            turn_out(prev[1])

            def attend(J, blk, last):
                off, N, p, bank = last
                e.wait_ge(m_done, val(p))
                for x in range(N // T + 1):
                    if x < N // T:
                        e.wait_ge(t_sb, val(bank + x) - (2 if off + x else 1))
                        for y in range(4):
                            a = x * T + y * P
                            m = e.transpose(ps[:, 4 + (off // T + x) % 2, y * P:y * P + P], scores[:, a:a + P], ident[:, :])
                        m.then_inc(t_ps, 1)
                    if x >= 1:
                        z = off // T + x - 1
                        e.wait_ge(t_sb, val(bank + x - 1))
                        if z == 0:
                            e.wait_ge(att_s, val(blk) - 1)
                        for y in range(4):
                            m = e.matmul(ps[:, 6, 0:P + 1], scoresT[:, (z % 4) * T + y * P:(z % 4) * T + y * P + P],
                                         tok[:, 4 * z + y, :], start=(z == 0 and y == 0), stop=(z == J - 1 and y == 3))
                        m.then_inc(o_mm, 1)

            def turn_out(blk):
                e.wait_ge(att_s, val(blk))
                e.transpose(ps[:, 7, 0:P], att, ident[:, :]).then_inc(at_ps, 1)

            def finish(prev):
                attend(*prev)
                turn_out(prev[1])

            walk_ahead(e, b, block_, finish)

        def act_attn(e, b):
            ln_act(e, b, cols(a_xn))
            for c in range(NCH):
                e.wait_ge(g_ps, of(b, c, NCH))
                e.activation(a_g[:, c * T:c * T + T], ps[:, 6 + c % 2, :], ACT.Identity, bias=b1c[:, :]).then_inc(g_rdy, 1)
            for c in range(NCH):
                e.wait_ge(tk_ps, of(b, c, NCH))
                e.activation(tok[:, 4 * c:4 * c + 4, 0:P], ps[:, c % 2, :].rearrange("p (a d) -> p a d", a=4),
                             ACT.Copy).then_inc(tk_rdy, 1)
            settled(e)
            e.preload_act_table_set("exp_and_others")
            e.wait_ge(g_rdy, of(b, NCH - 1, NCH))
            e.wait_ge(f_red, of(b, NCH - 1, NCH))

            def block_(J, r, blk, mine, prev):
                if prev:
                    e.wait_ge(th_done, val(prev[2][2], 16, 15))
                e.activation(row_bias[:, :], f_bias[:, ds(r * A16 + (J - 1) * 64, A16)], ACT.Copy).then_inc(rb_done, 1)
                e.wait_ge(rb_done, val(blk))
                for i, (off, N, p, bank) in enumerate(mine):
                    if i:
                        prev = (J, blk, mine[i - 1])
                    for u in range(4):
                        e.wait_ge(sc_mm, val(p, 4, u) - 2)
                        for c in range(4):
                            e.activation(tanh[(4 * u + c) % NT][:, 0:N], a_g[:, off:off + N], ACT.Tanh,
                                         bias=row_bias[:, 4 * c + u:4 * c + u + 1]).then_inc(th_done, 1)
                        if prev and u == 0:
                            exp(prev)

            def exp(prev):
                off, N, p, bank = prev[2]
                e.wait_ge(sc_mm, val(p, 4, 3))
                e.wait_ge(t_ps, val(bank) - 1)
                e.activation(scores[:, 0:N], ps[:, 0:N // T, :].rearrange("p a t -> p (a t)"), ACT.Exp,
                             bias=b2c[:, :]).then_inc(e_done, 1)

            walk_ahead(e, b, block_, exp)

        def dve_attn(e, b):
            ln_dve(e, b, cols(xT), cols(a_xn))
            e.memset(tok[:, :, P:P + 1], 1.0)
            for c in range(NCH):
                e.wait_ge(f_ps, of(b, c, NCH))
                if c >= 2:
                    e.wait_ge(f_red, of(b, c - 2, NCH))
                e.tensor_tensor(sel[:, c % 2, :].rearrange("p (a s) -> p a s", s=I8),
                                ps[:, 4 + c % 2, :].rearrange("p (a s) -> p a s", s=I8),
                                own[:, :].rearrange("p (o s) -> p o s", o=1).to_broadcast([P, T // I8, I8]), ALU.mult).then_inc(f_mul, 1)
                e.wait_ge(f_mul, of(b, c, NCH))
                e.reduce_sum(f_bias[:, c * (T // I8):(c + 1) * (T // I8)], sel[:, c % 2, :].rearrange("p (a s) -> p a s", s=I8),
                             axis=mybir.AxisListType.X).then_inc(f_red, 1)

            def block_(J, r, blk, mine):
                for i, (off, N, p, bank) in enumerate(mine):
                    for x in range(N // T):
                        e.wait_ge(t_ps, val(bank + x))
                        e.wait_ge(o_mm, val(bank + x) - 4)
                        y = off // T + x
                        e.tensor_copy(scoresT[:, (y % 4) * T:(y % 4) * T + T], ps[:, 4 + y % 2, :]).then_inc(t_sb, 1)
                e.wait_ge(o_mm, val(mine[-1][3] + (mine[-1][1] // T - 1)))
                e.wait_ge(at_add, val(blk) - 1)
                e.tensor_scalar(rden[:, 0:1], ps[:, 6, P:P + 1], 1e-10, None, ALU.add).then_inc(den_s, 1)
                e.wait_ge(den_s, val(blk, 2, 0))
                e.reciprocal(rden[:, 1:2], rden[:, 0:1]).then_inc(den_s, 1)
                e.wait_ge(den_s, val(blk, 2, 1))
                e.tensor_scalar(att, ps[:, 6, 0:P], rden[:, 1:2], None, ALU.mult).then_inc(att_s, 1)
                e.wait_ge(at_ps, val(blk))
                xb = xT[:, ds(r * P + (J - 1) * T, P)]
                e.tensor_tensor(xb, xb, ps[:, 7, 0:P], ALU.add).then_inc(at_add, 1)

            walk(e, b, block_)

        def pool_attn(e, b):
            def block_(J, r, blk, mine):
                for i, (off, N, p, bank) in enumerate(mine):
                    e.wait_ge(e_done, val(p))
                    if i == len(mine) - 1:
                        d = scores[:, N - T:N]
                        e.tensor_tensor(d, d, before[:, ds(3 * P - r * P, T)], ALU.mult).then_inc(m_done, 1)
                    else:
                        e.nop().then_inc(m_done, 1)

            walk(e, b, block_)

        B = batches
        logit = Y
        work = xT[:, :]
        df = dbu[:].rearrange("p a t -> p (a t)")
        pooled = df[:, 0:4 * E64].rearrange("p (b e) -> p b e", b=4)
        group_in = df[:, 2 * P:4 * P].rearrange("p (u e m) -> p u e m", u=2, e=EG)
        hid = [df[:, T + 128 * u:T + 128 * u + 64] for u in range(2)]
        hid_rows = Cs[:, 0:2, :]
        hidT = [Cs[:, 2 + u, :].rearrange("p (e c m) -> p e c m", e=EG, c=4) for u in range(2)]
        out_rows = df[:, 2 * T + 2 * P:2 * T + 4 * P].rearrange("p (u o) -> p u o", u=2)
        eout = df[:, 2 * T:2 * T + 2 * P].rearrange("p (a o) -> p a o", a=2)
        outT = df[:, 3 * T:3 * T + 4 * E64].rearrange("p (b e) -> p b e", b=4)
        slots = [Hf[:, 0:4 * T], Hf[:, 4 * T:8 * T], flat[1], scores]
        NGRP = E64 // EG

        def img(b):
            return V[:, b // 2, b % 2, :]

        def rows(pair):
            return E64 * min(2, B - 2 * pair)

        def w1s(u):
            return slots[2 * u].rearrange("p (e h) -> p e h", e=EG)

        def w2s(u):
            return slots[2 * u + 1].rearrange("p (e c o) -> p e c o", e=EG, c=4)

        def ehid(v):
            return v[:, 0:EG * 4 * B].rearrange("p (e c b) -> p e c b", e=EG, c=4)

        def steps(e, step):
            step((0, 0), None)
            settled(e)
            with e.Fori(0, NGRP // 2 - 1) as i:
                step((i, 1), (i, 0))
                step((i + 1, 0), (i, 1))
            step((NGRP // 2 - 1, 1), (NGRP // 2 - 1, 0))
            step(None, (NGRP // 2 - 1, 1))

        class PeTail:
            def norm(s, e, q, b):
                ln_pe(e, q, cols(xT))

            def logits(s, e, f):
                for b in range(B):
                    for c in range(NCH):
                        i = (f * B + b) * NCH + c
                        e.wait_ge(lg_rdy, val(i) - 2)
                        e.matmul(ps[E64 * (b % 2):E64 * (b % 2) + E64, c % 2, :], moe[f]["gw"], cols(img(b))(c),
                                 start=True, stop=True).then_inc(lg_ps, 1)

            def route(s, e, f):
                pass

            def pool(s, e, f):
                def turn(sb):
                    i = f * 32 + sb
                    e.wait_ge(c_tok, val(i) - 2)
                    for b in range(B):
                        m = e.transpose(ps[:, 4 + sb % 2, b * P:b * P + P], img(b)[:, sb * P:sb * P + P], ident[:, :])
                    m.then_inc(c_tok_ps, 1)
                    e.wait_ge(c_w, val(i) - 2)
                    for p in range((B + 1) // 2):
                        n = rows(p)
                        m = e.transpose(ps[:, 6 + sb % 2, p * P:p * P + n], logit[0:n, p, sb * P:sb * P + P], ident[0:n, 0:n])
                    m.then_inc(c_w_ps, 1)

                for sb in range(33):
                    if sb < 32:
                        turn(sb)
                    if sb == 0:
                        continue
                    x = sb - 1
                    e.wait_ge(c_tok, val(f * 32 + x))
                    e.wait_ge(c_w, val(f * 32 + x))
                    for b in range(B):
                        a = b * E64
                        m = e.matmul(ps[:, b, 0:E64], Cs[:, x % 2, b * P:b * P + P], Cs[:, 2 + x % 2, a:a + E64],
                                     start=(x == 0), stop=(x == 31))
                    m.then_inc(c_mm, 1)

            def experts(s, e, f):
                def step(h, o):
                    if h:
                        x2, u = h
                        g = 2 * x2 + u
                        i = g + f * NGRP
                        e.wait_ge(d_w1[u], x2 * 16 + (f * NGRP // 2 + 1) * 16)
                        e.wait_ge(d_in, val(i))
                        e.wait_ge(d_raw, val(i) - 2)
                        for x in range(EG):
                            m = e.matmul(ps[32 * x:32 * x + 32, 4 + u, :], group_in[:, u, x, :],
                                         w1s(u)[:, x, :], start=True, stop=True)
                        m.then_inc(d_h, 1)
                    if o:
                        x2, v = o
                        j = 2 * x2 + v + f * NGRP
                        e.wait_ge(d_w2[v], x2 * 16 + (f * NGRP // 2 + 1) * 16)
                        e.wait_ge(d_hT, val(j))
                        e.wait_ge(d_oc, val(j) - 2)
                        for c in range(4):
                            for x in range(EG):
                                m = e.matmul(ps[32 * x:32 * x + 32, 6 + v, 0:P], hidT[v][:, x, c, :], w2s(v)[:, x, c, :],
                                             start=(c == 0), stop=(c == 3))
                        m.then_inc(d_o, 1)
                    if h:
                        e.wait_ge(d_raw, val(i))
                        e.wait_ge(d_hb, val(i) - 2)
                        for c in range(4):
                            m = e.transpose(ps[:, u, c * P:c * P + P], hid_rows[:, u, c::4], ident[:, :])
                        m.then_inc(d_th, 1)
                    if o:
                        e.wait_ge(d_oc, val(j))
                        e.wait_ge(d_ot, val(j) - 2)
                        e.transpose(ps[:, 2 + v, 0:P], out_rows[:, v, :], ident[:, :]).then_inc(d_to, 1)

                steps(e, step)

            def outputs(s, e, f):
                for p in range((B + 1) // 2):
                    m = e.transpose(ps[0:rows(p), p, 0:P], outT[:, 2 * p:2 * p + rows(p) // E64, :].rearrange("p b e -> p (b e)"),
                                    ident[:, :])
                m.then_inc(o_t, 1)

            def scatter(s, e, f, b):
                a = E64 * (b % 2)
                for c in range(NCH):
                    i = (f * B + b) * NCH + c
                    e.wait_ge(f_add, val(i) - 2)
                    e.matmul(ps[:, 4 + c % 2, :], eout[a:a + E64, b // 2, :], logit[a:a + E64, b // 2, c * T:c * T + T],
                             start=True, stop=True).then_inc(f_ps2, 1)

            def attend(s, e, b):
                for c in range(NCH):
                    i = b * NCH + c
                    e.wait_ge(q_kv, val(i) - 2)
                    e.matmul(ps[:, 4 + c % 2, :], wk, cols(img(b))(c), start=True, stop=True)
                    e.matmul(ps[:, 6 + c % 2, :], wv, cols(img(b))(c), start=True, stop=True).then_inc(q_ps, 1)
                for c in range(NCH):
                    i = b * NCH + c
                    e.wait_ge(q_out, val(i) - 2)
                    e.matmul(ps[:, c % 2, :], wq, cols(img(b))(c), start=True, stop=True).then_inc(qq_ps, 1)

        class ActTail:
            def norm(s, e, q, b):
                ln_act(e, q, cols(img(b)))

            def logits(s, e, f):
                for b in range(B):
                    for c in range(NCH):
                        i = (f * B + b) * NCH + c
                        a = E64 * (b % 2)
                        e.wait_ge(lg_ps, val(i))
                        e.activation(logit[a:a + E64, b // 2, c * T:c * T + T], ps[a:a + E64, c % 2, :], ACT.Identity,
                                     bias=moe[f]["gb"][a:a + E64, :]).then_inc(lg_rdy, 1)

            def route(s, e, f):
                for p in range((B + 1) // 2):
                    n, i = rows(p), f * ((B + 1) // 2) + p
                    e.wait_ge(r_neg, val(i))
                    e.wait_ge(r_mark, val(i))
                    e.activation(logit[0:n, p, :], logit[0:n, p, :], ACT.Exp, bias=esum[0:n, p, 0:1],
                                 accum_out=esum[0:n, p, 1:2]).then_inc(r_exp, 1)

            def pool(s, e, f):
                for sb in range(32):
                    e.wait_ge(c_w_ps, val(f * 32 + sb))
                    if sb >= 2:
                        e.wait_ge(c_mm, val(f * 32 + sb) - 2)
                    e.activation(Cs[:, 2 + sb % 2, 0:E64 * B], ps[:, 6 + sb % 2, 0:E64 * B], ACT.Copy).then_inc(c_w, 1)

            def experts(s, e, f):
                settled(e)
                e.preload_act_table_set("gelu_and_others")

                def step(h, o):
                    if h:
                        u = h[1]
                        i = 2 * h[0] + u + f * NGRP
                        e.wait_ge(d_h, val(i))
                        e.wait_ge(d_th, val(i) - 2)
                        e.activation(hid_rows[:, u, :], ps[:, 4 + u, :], ACT.Copy).then_inc(d_raw, 1)
                    if o:
                        v = o[1]
                        j = 2 * o[0] + v + f * NGRP
                        e.wait_ge(d_o, val(j))
                        e.wait_ge(d_to, val(j) - 2)
                        e.activation(out_rows[:, v, :], ps[:, 6 + v, 0:P], ACT.Copy).then_inc(d_oc, 1)
                    if h:
                        e.wait_ge(d_hb, val(i))
                        e.wait_ge(d_o, val(i) - 2)
                        e.activation(hidT[u][:, :, :, 0:B], ehid(hid[u]), ACT.Gelu).then_inc(d_hT, 1)

                steps(e, step)
                settled(e)
                e.preload_act_table_set("natural_log_exp_and_others")

            def outputs(s, e, f):
                pass

            def scatter(s, e, f, b):
                pass

            def attend(s, e, b):
                for c in range(NCH):
                    e.wait_ge(q_ps, val(b * NCH + c))
                    e.wait_ge(q_kv, val(b * NCH + c) - 2)
                    e.activation(tmp[:, c % 2, 1, :], ps[:, 6 + c % 2, :], ACT.Identity, bias=qkvb[:, 2:3]).then_inc(q_v, 1)
                e.wait_ge(q_sum, val(b, 2, 1))
                for c in range(NCH):
                    e.wait_ge(qq_ps, val(b * NCH + c))
                    if c >= 2:
                        e.wait_ge(q_add, val(b * NCH + c) - 2)
                    e.activation(tmp[:, c % 2, 1, :], ps[:, c % 2, :], ACT.Identity, scale=kvs[:, NCH:NCH + 1],
                                 bias=kvs[:, NCH + 1:NCH + 2]).then_inc(q_out, 1)

        class DveTail:
            def norm(s, e, q, b):
                ln_dve(e, q, cols(xT), cols(img(b)))

            def logits(s, e, f):
                pass

            def route(s, e, f):
                for p in range((B + 1) // 2):
                    n, i = rows(p), f * ((B + 1) // 2) + p
                    x = logit[0:n, p, :]
                    e.max(top8[0:n, p, :], x).then_inc(r_max, 1)
                    e.wait_ge(r_max, val(i))
                    if p:
                        e.wait_ge(r_w, val(i) - 1)
                    e.tensor_scalar(esum[0:n, p, 0:1], top8[0:n, p, 0:1], -1.0, None, ALU.mult).then_inc(r_neg, 1)
                    e.match_replace(work[0:n, :], top8[0:n, p, :], x, LOWEST).then_inc(r_mark, 1)
                    e.wait_ge(r_mark, val(i))
                    e.wait_ge(r_exp, val(i))
                    e.reciprocal(esum[0:n, p, 2:3], esum[0:n, p, 1:2]).then_inc(r_inv, 1)
                    e.scalar_tensor_tensor(x, work[0:n, :], LOWEST, x, ALU.is_le, ALU.mult).then_inc(r_w, 1)
                    e.wait_ge(r_inv, val(i))
                    e.wait_ge(r_w, val(i))
                    e.tensor_scalar(x, x, esum[0:n, p, 2:3], None, ALU.mult).then_inc(r_scaled, 1)

            def pool(s, e, f):
                e.memset(group_in[:, :, :, :], 0.0).then_inc(c_out, 1)
                for sb in range(32):
                    e.wait_ge(c_tok_ps, val(f * 32 + sb))
                    if sb >= 2:
                        e.wait_ge(c_mm, val(f * 32 + sb) - 2)
                    e.tensor_copy(Cs[:, sb % 2, 0:P * B], ps[:, 4 + sb % 2, 0:P * B]).then_inc(c_tok, 1)
                e.wait_ge(c_mm, val(f * 32 + 31))
                e.wait_ge(c_out, val(f, 2, 0))
                e.tensor_copy(pooled[:, 0:B, :], ps[:, 0:B, 0:E64]).then_inc(c_out, 1)
                e.memset(Cs[:, 2:4, :], 0.0)

            def experts(s, e, f):
                def step(h, o):
                    if h:
                        g, u = 2 * h[0] + h[1], h[1]
                        i = g + f * NGRP
                        e.wait_ge(d_h, val(i) - 2)
                        e.tensor_copy(group_in[:, u, :, 0:B], pooled[:, 0:B, ds(EG * g, EG)].rearrange("p b e -> p e b")).then_inc(d_in, 1)
                        e.wait_ge(d_th, val(i))
                        e.wait_ge(d_hT, val(i) - 2)
                        b1 = moe[f]["b1"][:, :, ds(EG * g, EG)].rearrange("p c (e o) -> p e c o", o=1)
                        e.tensor_tensor(ehid(hid[u]), ps[:, u, :].rearrange("p (c x m) -> p x c m", c=4, x=EG)[:, :, :, 0:B],
                                        b1.to_broadcast([P, EG, 4, B]), ALU.add).then_inc(d_hb, 1)
                    if o:
                        g, v = 2 * o[0] + o[1], o[1]
                        e.wait_ge(d_to, val(g + f * NGRP))
                        e.tensor_copy(outT[:, 0:B, ds(EG * g, EG)],
                                      ps[:, 2 + v, 0:P].rearrange("p (x m) -> p m x", x=EG)[:, 0:B, :]).then_inc(d_ot, 1)

                steps(e, step)

            def outputs(s, e, f):
                e.wait_ge(o_t, val(f))
                for p in range((B + 1) // 2):
                    n = rows(p)
                    e.tensor_tensor(eout[0:n, p, :], ps[0:n, p, 0:P], moe[f]["b2"][0:n, :], ALU.add).then_inc(o_b, 1)

            def scatter(s, e, f, b):
                for c in range(NCH):
                    x = cols(xT)(c)
                    e.wait_ge(f_ps2, val((f * B + b) * NCH + c))
                    e.tensor_tensor(x, x, ps[:, 4 + c % 2, :], ALU.add).then_inc(f_add, 1)

            def attend(s, e, b):
                for c in range(NCH):
                    i = b * NCH + c
                    e.wait_ge(q_v, val(i))
                    v = tmp[:, c % 2, 1, :]
                    e.scalar_tensor_tensor(v, ps[:, 4 + c % 2, :], qkvb[:, 1:2], v, ALU.add, ALU.mult,
                                           accum_out=kvs[:, c:c + 1]).then_inc(q_kv, 1)
                e.wait_ge(q_kv, val(b * NCH + NCH - 1))
                e.reduce_sum(kvs[:, NCH:NCH + 1], kvs[:, 0:NCH], axis=mybir.AxisListType.X).then_inc(q_sum, 1)
                e.wait_ge(q_sum, val(b, 2, 0))
                e.tensor_tensor(kvs[:, NCH + 1:NCH + 2], kvs[:, NCH:NCH + 1], qkvb[:, 0:1], ALU.mult).then_inc(q_sum, 1)
                for c in range(NCH):
                    e.wait_ge(q_out, val(b * NCH + c))
                    x = cols(xT)(c)
                    e.tensor_tensor(x, x, tmp[:, c % 2, 1, :], ALU.add).then_inc(q_add, 1)

        class PoolTail:
            def norm(s, e, q, b):
                pass

            logits = route = pool = experts = outputs = lambda s, e, f: None

            def scatter(s, e, f, b):
                pass

            def attend(s, e, b):
                pass

        class SyncTail(PoolTail):
            def experts(s, e, f):
                m = f + 2

                def load(g, u):
                    i = g + f * NGRP
                    e.wait_ge(d_h, val(i) - 2)
                    e.dma_start(slots[2 * u].rearrange("p (e h) -> p e h", e=EG),
                                t[f"u1_{m}"][ds(EG * g, EG), 0:P, :].rearrange("e d h -> d e h")).then_inc(d_w1[u], 16)
                    e.wait_ge(d_o, val(i) - 2)
                    e.dma_start(slots[2 * u + 1].rearrange("p (e h) -> p e h", e=EG),
                                t[f"u2_{m}"][ds(EG * g, EG), 0:HID, :].rearrange("e (p c) o -> p e (c o)", c=4)).then_inc(d_w2[u], 16)

                with e.Fori(0, NGRP // 2) as i:
                    load(2 * i, 0)
                    load(2 * i + 1, 1)

        def tail(e, x, load, store):
            n = [B * (NSTG + 2)]

            def end():
                barrier(e, n[0])
                n[0] += 1

            load("weights", 0)
            for b in range(B):
                load("x", b)
                end()
                x.norm(e, B + b, b)
                end()
            for f in range(2):
                x.logits(e, f)
                end()
                x.route(e, f)
                end()
                x.pool(e, f)
                end()
                x.experts(e, f)
                end()
                x.outputs(e, f)
                end()
                for b in range(B):
                    load("x", b)
                    end()
                    x.scatter(e, f, b)
                    end()
                    if f == 0:
                        x.norm(e, 2 * B + 2 * b, b)
                        end()
                        x.attend(e, b)
                        end()
                        store(res, b)
                        x.norm(e, 2 * B + 2 * b + 1, b)
                        end()
                    else:
                        store(out, b)
                        end()

        NSTG = 7

        @block.sync
        def _(e):
            n = 0
            for ly, w in enumerate(lay):
                for name in ("win", "cw", "cb", "dtb", "al", "dd", "lw", "lb", "wo"):
                    e.dma_start(w[name][:], t[f"{name}{ly}"]).then_inc(s_w, 16)
                    n += 1
                for i in range(3):
                    e.dma_start(w["wx"][:, :, :, 32 * i:32 * i + 32], t[f"wx{ly}"][:, :, :, R:]).then_inc(s_w, 16)
                e.dma_start(w["wx"][:, :, :, NSPLIT:], t[f"wx{ly}"][:, :, :, 0:R]).then_inc(s_w, 16)
                e.dma_start(w["wdt"][NSPLIT:], t[f"wdt{ly}"]).then_inc(s_w, 16)
                n += 5
            for dst, name in ((w1f, "w1f"), (w1g, "w1g"), (b1c, "b1c"), (w2c, "w2c"), (b2c, "b2c")):
                e.dma_start(dst[:], t[name]).then_inc(s_w, 16)
                n += 1
            assert n == N_WEIGHTS
            with e.Fori(0, batches) as b:
                e.dma_start(xT[:], t["xT"][ds(b, 1)].rearrange("a p l -> (a p) l")).then_inc(s_x, 16)
                e.wait_ge(s_x, b * 16 + 16)
                settled(e)
                barrier(e, b * (NSTG + 2))
                for ly in range(2):
                    for i in range(3):
                        barrier(e, b * (NSTG + 2) + (1 + 3 * ly + i))
                barrier(e, b * (NSTG + 2) + NSTG)
                e.dma_start(res[ds(b, 1)].rearrange("a p l -> (a p) l"), xT[:]).then_inc(s_store, 16)
                e.wait_ge(s_store, b * 16 + 16)
                settled(e)
                barrier(e, b * (NSTG + 2) + (NSTG + 1))

            loads = [B * 16]

            def load(what, b):
                if what == "weights":
                    for dst, name in ((wq, "wq"), (wk, "wk"), (wv, "wv"), (qkvb, "qkvb")):
                        e.dma_start(dst, t[name]).then_inc(s_w, 16)
                    for m, w in zip((2, 3), moe):
                        for name in ("gw", "gb", "b1", "b2"):
                            e.dma_start(w[name], t[f"{name}_{m}"]).then_inc(s_w, 16)
                    e.wait_ge(s_w, 16 * (N_WEIGHTS + 12))
                else:
                    e.dma_start(xT[:], res[b]).then_inc(s_x, 16)
                    loads[0] += 16
                    e.wait_ge(s_x, loads[0])

            stored = [B * 16]

            def store(dst, b):
                e.dma_start(dst[b], xT[:]).then_inc(s_store, 16)
                stored[0] += 16
                e.wait_ge(s_store, stored[0])

            tail(e, SyncTail(), load, store)

        @block.gpsimd
        def _(e):
            e.memset(ident[:], 0.0).then_inc(s_const, 1)
            e.memset(group_mean[:], 0.25).then_inc(s_const, 1)
            e.memset(mean256[:], 1.0 / DI)
            e.memset(mean128[:], 1.0 / P)
            e.memset(pick[:], 0.0).then_inc(s_const, 1)
            e.memset(keep_mid[:], -1.0)
            e.memset(keep_low[:], -1.0).then_inc(s_const, 1)
            e.memset(eps[:, 0:1], 1e-5).then_inc(s_const, 1)
            e.memset(eps[:, 1:2], 1e-10).then_inc(s_const, 1)
            e.memset(before[:], 1.0)
            e.memset(own[:], 1.0)
            e.memset(w2pick[:], 0.0).then_inc(s_const, 1)
            for s in counting:
                e.nop().then_inc(s, CR)
            e.wait_ge(s_const, 7)
            e.affine_select(out=ident[:], in_=ident[:], compare_op=ALU.not_equal, fill=1.0, base=0,
                            pattern=[[-1, P]], channel_multiplier=1).then_inc(s_const, 1)
            gm = group_mean[:].rearrange("p (g m) -> p g m", m=4)
            e.affine_select(out=gm, in_=gm, compare_op=ALU.is_ge, fill=0.0, base=0,
                            pattern=[[-4, 32], [0, 4]], channel_multiplier=1).then_inc(s_const, 1)
            e.affine_select(out=keep_mid[:], in_=keep_mid[:], compare_op=ALU.is_ge, fill=0.0, base=-32,
                            pattern=[[0, 1]], channel_multiplier=1)
            e.affine_select(out=keep_low[:], in_=keep_low[:], compare_op=ALU.is_ge, fill=0.0, base=-64,
                            pattern=[[0, 1]], channel_multiplier=1).then_inc(s_const, 1)
            e.affine_select(out=own[:], in_=own[:], compare_op=ALU.is_ge, fill=0.0, base=0,
                            pattern=[[-A16, I8]], channel_multiplier=1).then_inc(s_const, 1)
            e.affine_select(out=before[:], in_=before[:], compare_op=ALU.is_gt, fill=0.0, base=3 * P,
                            pattern=[[-1, T + 3 * P]], channel_multiplier=1).then_inc(s_const, 1)
            e.wait_ge(s_const, 12)
            e.affine_select(out=own[:], in_=own[:], compare_op=ALU.is_ge, fill=0.0, base=A16 - 1,
                            pattern=[[A16, I8]], channel_multiplier=-1).then_inc(s_const, 1)
            e.affine_select(out=gm, in_=gm, compare_op=ALU.is_ge, fill=0.0, base=3,
                            pattern=[[4, 32], [0, 4]], channel_multiplier=-1).then_inc(s_const, 1)
            for i in range(3):
                e.affine_select(out=pick[:], in_=pick[:], compare_op=ALU.not_equal, fill=1.0, base=-32 * i,
                                pattern=[[-1, 32]], channel_multiplier=1).then_inc(s_const, 1)
                e.wait_ge(s_const, 15 + i)
            x = Pool(e)
            with e.Fori(0, batches) as b:
                barrier(e, b * (NSTG + 2))
                for ly in range(2):
                    barrier(e, b * (NSTG + 2) + (1 + 3 * ly))
                    x.pre(ly, first(ly, b))
                    chunks(e, ly, b, lambda k, c, it, par, nx, prev, last: x.main(it, par, nx))
                    barrier(e, b * (NSTG + 2) + (2 + 3 * ly))
                    barrier(e, b * (NSTG + 2) + (3 + 3 * ly))
                pool_attn(e, b)
                barrier(e, b * (NSTG + 2) + NSTG)
                barrier(e, b * (NSTG + 2) + (NSTG + 1))
            tail(e, PoolTail(), lambda *a: None, lambda *a: None)

        @block.vector
        def _(e):
            e.wait_ge(s_w, 16 * N_WEIGHTS)
            for ly, w in enumerate(lay):
                e.tensor_scalar(w["al"][:], w["al"][:], 85.0, None, ALU.min).then_inc(s_aexp, 1)
                kk = w["kk"]
                for d in range(2):
                    i = e.tensor_tensor(w["dsum"][:, d, :], w["dd"][:, d % kk, :], w["dd"][:, (d + 2) % kk, :], ALU.add)
                i.then_inc(s_aexp, 1)
            e.wait_ge(s_const, 17)
            for u in range(4):
                e.tensor_scalar(w2pick[:, u, 8 * u:8 * u + 8], own[:, :], w2c[:, :], None, ALU.mult)
            e.tensor_scalar(take_high[:, :], ident[0:NSPLIT, 0:NSPLIT], keep_mid[:, :], None, ALU.mult)
            e.tensor_scalar(take_mid[:, :], ident[0:NSPLIT, 0:NSPLIT], keep_low[:, :], None, ALU.mult)
            e.wait_ge(s_aexp, 6)
            for ly, w in enumerate(lay):
                e.tensor_scalar(w["na"][:], w["na"][:], -1.0, None, ALU.mult).then_inc(s_aexp, 1)
            x = Dve(e)
            with e.Fori(0, batches) as b:
                barrier(e, b * (NSTG + 2))
                for ly in range(2):
                    dve_front(e, ly, b * 2 + ly)
                    barrier(e, b * (NSTG + 2) + (1 + 3 * ly))
                    x.pre(ly, first(ly, b))
                    chunks(e, ly, b, lambda k, c, it, par, nx, prev, last: x.main(ly, it, par, nx, last))
                    barrier(e, b * (NSTG + 2) + (2 + 3 * ly))
                    dve_back(e, ly, b * 2 + ly)
                    barrier(e, b * (NSTG + 2) + (3 + 3 * ly))
                dve_attn(e, b)
                barrier(e, b * (NSTG + 2) + NSTG)
                barrier(e, b * (NSTG + 2) + (NSTG + 1))
            tail(e, DveTail(), lambda *a: None, lambda *a: None)

        @block.scalar
        def _(e):
            settled(e)
            e.preload_act_table_set("natural_log_exp_and_others")
            e.wait_ge(s_aexp, 4)
            for ly, w in enumerate(lay):
                e.activation(w["na"][:], w["al"][:], ACT.Exp).then_inc(s_aexp, 1)
            x = Act(e)
            with e.Fori(0, batches) as b:
                barrier(e, b * (NSTG + 2))
                for ly in range(2):
                    act_front(e, ly, b * 2 + ly)
                    settled(e)
                    e.preload_act_table_set("natural_log_exp_and_others")
                    barrier(e, b * (NSTG + 2) + (1 + 3 * ly))
                    x.pre(ly, first(ly, b))
                    base = chunks(e, ly, b, lambda k, c, it, par, nx, prev, last: x.main(ly, it, par, k, nx, prev))
                    x.keep_y((K - 1, NCH - 1, base + (K * NCH - 1)))
                    barrier(e, b * (NSTG + 2) + (2 + 3 * ly))
                    act_back(e, ly, b * 2 + ly)
                    barrier(e, b * (NSTG + 2) + (3 + 3 * ly))
                act_attn(e, b)
                barrier(e, b * (NSTG + 2) + NSTG)
                settled(e)
                e.preload_act_table_set("natural_log_exp_and_others")
                barrier(e, b * (NSTG + 2) + (NSTG + 1))
            tail(e, ActTail(), lambda *a: None, lambda *a: None)

        @block.tensor
        def _(e):
            e.wait_ge(s_w, 16 * N_WEIGHTS)
            x = Pe(e)
            with e.Fori(0, batches) as b:
                barrier(e, b * (NSTG + 2))
                for ly in range(2):
                    pe_front(e, ly, b * 2 + ly)
                    barrier(e, b * (NSTG + 2) + (1 + 3 * ly))
                    x.pre(ly, first(ly, b))
                    chunks(e, ly, b, lambda k, c, it, par, nx, prev, last: x.main(ly, k, c, it, par, nx))
                    barrier(e, b * (NSTG + 2) + (2 + 3 * ly))
                    pe_back(e, ly, b * 2 + ly)
                    barrier(e, b * (NSTG + 2) + (3 + 3 * ly))
                pe_attn(e, b)
                barrier(e, b * (NSTG + 2) + NSTG)
                barrier(e, b * (NSTG + 2) + (NSTG + 1))
            tail(e, PeTail(), lambda *a: None, lambda *a: None)


N_WEIGHTS = 2 * 14 + 5


def kernel(**inputs):
    import numpy as np
    import concourse.bacc as _bacc
    from concourse import mybir as _mybir
    from concourse.bass_utils import run_bass_kernel_spmd as _run

    i = {k: np.asarray(v) for k, v in inputs.items()}
    B = i["x"].shape[0]

    def halves(a):
        return a.reshape(a.shape[0], 2, P, -1).transpose(2, 0, 1, 3)

    a = {"xT": i["x"].reshape(B, L, P).transpose(0, 2, 1)}
    c0, c1 = "L0_conv_", "L1_conv_"
    a["win0"], a["win1"] = i[c0 + "w_in"], i[c1 + "W_in"].T
    a["cw0"] = halves(i[c0 + "conv_w"].reshape(1, 9, DI).transpose(0, 2, 1))[:, 0]
    a["cw1"] = halves(i[c1 + "conv_w"].reshape(1, DI, 9))[:, 0]
    a["wx0"] = halves(i[c0 + "w_xproj"][None])
    a["wx1"] = halves(i[c1 + "x_proj_w"].transpose(0, 2, 1))
    a["wdt0"] = i[c0 + "w_dt"][:, None, :]
    a["wdt1"] = i[c1 + "dt_proj_w"].transpose(2, 0, 1)
    a["al0"], a["al1"] = halves(i[c0 + "A_log"][None]), halves(i[c1 + "A_logs"].reshape(K, DI, NS))
    a["dtb0"], a["dtb1"] = halves(i[c0 + "b_dt"][None])[..., 0], halves(i[c1 + "dt_proj_b"])[..., 0]
    a["dd0"], a["dd1"] = halves(i[c0 + "D_param"][None])[..., 0], halves(i[c1 + "Ds"].reshape(K, DI))[..., 0]
    for n, c in ((0, c0), (1, c1)):
        a[f"cb{n}"] = halves(i[c + "conv_b"][None])[:, 0, :, 0]
        a[f"lw{n}"] = halves(i[c + "ln_w"][None])[:, 0, :, 0]
        a[f"lb{n}"] = halves(i[c + "ln_b"][None])[:, 0, :, 0]
    a["wo0"] = halves(i[c0 + "w_out"][None])[:, 0]
    a["wo1"] = halves(i[c1 + "W_out"].T[None])[:, 0]

    def rep(v):
        return np.broadcast_to(v[..., None, :], v.shape[:-1] + (I8, A16)).reshape(v.shape[:-1] + (P,))

    w1 = i["L2_attn_W1"]
    a["w1f"], a["w1g"] = rep(w1[:P]), rep(w1[P:])
    a["b1c"], a["w2c"] = rep(i["L2_attn_b1"])[:, None], rep(i["L2_attn_w2"][:, 0])[:, None]
    a["b2c"] = np.broadcast_to(i["L2_attn_b2"][None], (P, 1))
    a["wq"], a["wk"], a["wv"] = i["L3_attn_Wq"], i["L3_attn_Wk"], i["L3_attn_Wv"]
    a["qkvb"] = np.stack([i["L3_attn_bq"], i["L3_attn_bk"], i["L3_attn_bv"]], axis=1)
    for m in (2, 3):
        c = f"L{m}_ffn_"
        u1, u2 = i[c + "weight1"], i[c + "weight2"]
        a[f"gw_{m}"] = i[c + "gate_w"].T
        a[f"gb_{m}"] = np.concatenate([i[c + "gate_b"]] * 2)[:, None]
        a[f"b1_{m}"] = u1[:, P].reshape(E64, P, 4).transpose(1, 2, 0)
        a[f"b2_{m}"] = np.concatenate([u2[:, HID]] * 2)
        a[f"u1_{m}"], a[f"u2_{m}"] = u1, u2

    nc = _bacc.Bacc("TRN2", target_bir_lowering=False, num_devices=1)
    arrays, t = {}, {}
    for name, v in a.items():
        v = np.ascontiguousarray(v)
        arrays[f"in_{name}_dram"] = v
        t[name] = nc.dram_tensor(f"in_{name}_dram", v.shape, _mybir.dt.from_np(v.dtype), kind="ExternalInput").ap()
    out = nc.dram_tensor("out_0_dram", (B, P, L), _mybir.dt.float32, kind="ExternalOutput").ap()
    res = nc.dram_tensor("residual_dram", (B, P, L), _mybir.dt.float32, kind="Internal").ap()
    program(nc, t, res, out, B)
    r = _run(nc, [arrays], core_ids=[0])
    return r.results[0]["out_0_dram"].reshape(B, P, W, W).transpose(0, 2, 3, 1)
```
